# Optimizing a Trainium2 kernel written in Bass

```python
import numpy as np
import jax
import jax.numpy as jnp

def _softmax(x, axis=-1):
    return jax.nn.softmax(x, axis=axis)

def _gelu(x):
    return jax.nn.gelu(x, approximate=True)

def _silu(x):
    return jax.nn.silu(x)

def _sigmoid(x):
    return jax.nn.sigmoid(x)

def _layernorm(x, axis=-1, eps=1e-05):
    m = jnp.mean(x, axis=axis, keepdims=True)
    v = jnp.var(x, axis=axis, keepdims=True)
    return (x - m) / jnp.sqrt(v + eps)

def _scatter_add(tgt, idx, src, axis=0):
    return tgt.at[idx].add(src)

def _segment_sum(src, seg, n):
    return jax.ops.segment_sum(src, seg, n)
kernel_name = 'mk_conv_preact_d4_conv_nchw64_r2_196aa5'

def setup_inputs(seed: int=0):
    np.random.seed(seed)
    _w = jnp.asarray

    def _rec_inputs():
        import jax
        import jax.numpy as jnp
        _gk = jax.random.key(seed)
        x = -0.0002928 + 1 * jax.random.normal(jax.random.fold_in(_gk, 1), (4, 32, 64, 64), jnp.float32)
        return x
    x = _rec_inputs()

    def _L0_conv_setup():
        import jax, jax.numpy as jnp
        import numpy as np
        K = 3
        PAD = 1
        GROUPS = 1
        BASES = 16

        def _conv2d(x, w, b, pad):
            out = jax.lax.conv_general_dilated(x, w, window_strides=(1, 1), padding=[(pad, pad), (pad, pad)], dimension_numbers=('NCHW', 'OIHW', 'NCHW'))
            return out + b[None, :, None, None]
        key = jax.random.key(seed)
        ks = jax.random.split(key, 5)
        B, C, H, Wd = (4, 32, 64, 64)
        x = jax.random.normal(ks[0], (B, C, H, Wd), dtype=jnp.float32)
        J = C // GROUPS * K * K
        Og = C // GROUPS
        W = jax.random.normal(ks[1], (1, GROUPS, Og * J, BASES), dtype=jnp.float32) * 0.05
        pw = jax.random.normal(ks[2], (BASES, C, 1, 1), dtype=jnp.float32) * 0.05
        pb = jnp.zeros((BASES,), dtype=jnp.float32)
        cw = jax.random.normal(ks[3], (BASES, BASES, 3, 3), dtype=jnp.float32) * 0.05
        cb = jnp.zeros((BASES,), dtype=jnp.float32)
        return {'x': x, 'W': W, 'pw': pw, 'pb': pb, 'cw': cw, 'cb': cb}
    _L0_conv_all = _L0_conv_setup()
    _L0_conv_in = {k: v for k, v in _L0_conv_all.items() if k in ('W', 'pw', 'pb', 'cw', 'cb')}
    del _L0_conv_all

    def _L1_conv_setup():
        import jax, jax.numpy as jnp
        import numpy as np
        STRIDE = 1
        PAD = 1
        EXTENT = 3

        def _bilinear_tap(xp, dy, dx, H_out, W_out):
            Hp, Wp = (xp.shape[-2], xp.shape[-1])
            y = jnp.arange(H_out, dtype=xp.dtype) * STRIDE + dy
            xc = jnp.arange(W_out, dtype=xp.dtype) * STRIDE + dx
            y0 = jnp.floor(y)
            x0 = jnp.floor(xc)
            fy = (y - y0)[None, None, :, None]
            fx = (xc - x0)[None, None, None, :]
            y0i = jnp.clip(y0.astype(jnp.int32), 0, Hp - 1)
            y1i = jnp.clip(y0.astype(jnp.int32) + 1, 0, Hp - 1)
            x0i = jnp.clip(x0.astype(jnp.int32), 0, Wp - 1)
            x1i = jnp.clip(x0.astype(jnp.int32) + 1, 0, Wp - 1)
            ry = xp[:, :, y0i, :] * (1.0 - fy) + xp[:, :, y1i, :] * fy
            return ry[:, :, :, x0i] * (1.0 - fx) + ry[:, :, :, x1i] * fx
        key = jax.random.key(seed)
        k1, k2 = jax.random.split(key)
        B, Cin, H, W = (8, 32, 64, 64)
        Cout, K = (32, 9)
        x = jax.random.normal(k1, (B, Cin, H, W), dtype=jnp.float32)
        weights = jax.random.normal(k2, (Cout, Cin, K), dtype=jnp.float32) * 0.05
        base = jnp.stack(jnp.meshgrid(jnp.arange(3.0), jnp.arange(3.0), indexing='ij'), -1).reshape(9, 2)
        tap_offsets = (base + 0.4).astype(jnp.float32)
        return {'x': x, 'weights': weights, 'tap_offsets': tap_offsets}
    _L1_conv_all = _L1_conv_setup()
    _L1_conv_in = {k: v for k, v in _L1_conv_all.items() if k in ('weights', 'tap_offsets')}
    del _L1_conv_all

    def _L2_conv_setup():
        import jax, jax.numpy as jnp
        import numpy as np
        from jax import lax
        E, C, COUT, P, K = (4, 32, 32, 4, 16)
        B, H, W = (32, 56, 56)
        EPS = 1e-05

        def _conv(x, w, stride=1, pad=0):
            return lax.conv_general_dilated(x, w, (stride, stride), ((pad, pad), (pad, pad)), dimension_numbers=('NCHW', 'OIHW', 'NCHW'))

        def _bn(x, gamma, beta):
            mean = jnp.mean(x, axis=(0, 2, 3), keepdims=True)
            var = jnp.var(x, axis=(0, 2, 3), keepdims=True)
            xn = (x - mean) * lax.rsqrt(var + EPS)
            return gamma[None, :, None, None] * xn + beta[None, :, None, None]

        def _gate(x, k1, k2):
            g = _conv(x, k1, stride=P)
            g = _conv(g, k2)
            g = jax.nn.softmax(g, axis=1)
            b, _, h, w = g.shape
            flat = g.reshape(b, h * w)
            vals, idx = lax.top_k(flat, K)
            ret = jnp.zeros_like(flat).at[jnp.arange(b)[:, None], idx].add(vals)
            m = ret.reshape(b, 1, h, w)
            m = jnp.repeat(jnp.repeat(m, P, axis=2), P, axis=3)
            return x * m
        key = jax.random.key(seed)
        ks = jax.random.split(key, 8)
        x = jax.random.normal(ks[0], (B, C, H, W), dtype=jnp.float32)
        gk1 = jax.random.normal(ks[1], (E, C // 2, C, P, P), dtype=jnp.float32) * 0.0001
        gk2 = jax.random.normal(ks[2], (E, 1, C // 2, 1, 1), dtype=jnp.float32) * 0.0001
        w1 = jax.random.normal(ks[3], (E, COUT, C, 3, 3), dtype=jnp.float32) * 0.05
        b1 = jax.random.normal(ks[4], (E, COUT), dtype=jnp.float32) * 0.01
        w2 = jax.random.normal(ks[5], (E, COUT, COUT, 3, 3), dtype=jnp.float32) * 0.05
        b2 = jax.random.normal(ks[6], (E, COUT), dtype=jnp.float32) * 0.01
        gamma1 = jnp.ones((E, COUT), dtype=jnp.float32)
        beta1 = jnp.zeros((E, COUT), dtype=jnp.float32)
        gamma2 = jnp.ones((E, COUT), dtype=jnp.float32)
        beta2 = jnp.zeros((E, COUT), dtype=jnp.float32)
        return {'x': x, 'gk1': gk1, 'gk2': gk2, 'w1': w1, 'b1': b1, 'gamma1': gamma1, 'beta1': beta1, 'w2': w2, 'b2': b2, 'gamma2': gamma2, 'beta2': beta2}
    _L2_conv_all = _L2_conv_setup()
    _L2_conv_in = {k: v for k, v in _L2_conv_all.items() if k in ('gk1', 'gk2', 'w1', 'b1', 'gamma1', 'beta1', 'w2', 'b2', 'gamma2', 'beta2')}
    del _L2_conv_all

    def _L3_conv_setup():
        import jax, jax.numpy as jnp
        import numpy as np
        EPS = 1e-05

        def _conv3x3(x, w):
            return jax.lax.conv_general_dilated(x, w, window_strides=(1, 1), padding=((1, 1), (1, 1)), dimension_numbers=('NCHW', 'OIHW', 'NCHW'))

        def _bn(x, gamma, beta, mean, var):
            inv = gamma / jnp.sqrt(var + EPS)
            return x * inv[None, :, None, None] + (beta - mean * inv)[None, :, None, None]
        key = jax.random.key(seed)
        ks = jax.random.split(key, 6)
        B, C, H, W, E = (32, 32, 56, 56, 10)
        x = jax.random.normal(ks[0], (B, C, H, W), dtype=jnp.float32)
        w1 = jax.random.normal(ks[1], (E, C, C, 3, 3), dtype=jnp.float32) * 0.05
        w2 = jax.random.normal(ks[2], (E, C, C, 3, 3), dtype=jnp.float32) * 0.05
        alpha = jax.random.uniform(ks[3], (E,), dtype=jnp.float32)
        return {'x': x, 'w1': w1, 'w2': w2, 'alpha': alpha, 'bn1_gamma': jnp.ones((C,), jnp.float32), 'bn1_beta': jnp.zeros((C,), jnp.float32), 'bn1_mean': jnp.zeros((C,), jnp.float32), 'bn1_var': jax.random.uniform(ks[4], (C,), jnp.float32) + 0.5, 'bn2_gamma': jnp.ones((C,), jnp.float32), 'bn2_beta': jnp.zeros((C,), jnp.float32), 'bn2_mean': jnp.zeros((C,), jnp.float32), 'bn2_var': jax.random.uniform(ks[5], (C,), jnp.float32) + 0.5}
    _L3_conv_all = _L3_conv_setup()
    _L3_conv_in = {k: v for k, v in _L3_conv_all.items() if k in ('w1', 'w2', 'alpha', 'bn1_gamma', 'bn1_beta', 'bn1_mean', 'bn1_var', 'bn2_gamma', 'bn2_beta', 'bn2_mean', 'bn2_var')}
    del _L3_conv_all
    return {'x': x, 'L0_conv_W': _L0_conv_in['W'], 'L0_conv_pw': _L0_conv_in['pw'], 'L0_conv_pb': _L0_conv_in['pb'], 'L0_conv_cw': _L0_conv_in['cw'], 'L0_conv_cb': _L0_conv_in['cb'], 'L1_conv_weights': _L1_conv_in['weights'], 'L1_conv_tap_offsets': _L1_conv_in['tap_offsets'], 'L2_conv_gk1': _L2_conv_in['gk1'], 'L2_conv_gk2': _L2_conv_in['gk2'], 'L2_conv_w1': _L2_conv_in['w1'], 'L2_conv_b1': _L2_conv_in['b1'], 'L2_conv_gamma1': _L2_conv_in['gamma1'], 'L2_conv_beta1': _L2_conv_in['beta1'], 'L2_conv_w2': _L2_conv_in['w2'], 'L2_conv_b2': _L2_conv_in['b2'], 'L2_conv_gamma2': _L2_conv_in['gamma2'], 'L2_conv_beta2': _L2_conv_in['beta2'], 'L3_conv_w1': _L3_conv_in['w1'], 'L3_conv_w2': _L3_conv_in['w2'], 'L3_conv_alpha': _L3_conv_in['alpha'], 'L3_conv_bn1_gamma': _L3_conv_in['bn1_gamma'], 'L3_conv_bn1_beta': _L3_conv_in['bn1_beta'], 'L3_conv_bn1_mean': _L3_conv_in['bn1_mean'], 'L3_conv_bn1_var': _L3_conv_in['bn1_var'], 'L3_conv_bn2_gamma': _L3_conv_in['bn2_gamma'], 'L3_conv_bn2_beta': _L3_conv_in['bn2_beta'], 'L3_conv_bn2_mean': _L3_conv_in['bn2_mean'], 'L3_conv_bn2_var': _L3_conv_in['bn2_var']}

def reference(x, L0_conv_W, L0_conv_pw, L0_conv_pb, L0_conv_cw, L0_conv_cb, L1_conv_weights, L1_conv_tap_offsets, L2_conv_gk1, L2_conv_gk2, L2_conv_w1, L2_conv_b1, L2_conv_gamma1, L2_conv_beta1, L2_conv_w2, L2_conv_b2, L2_conv_gamma2, L2_conv_beta2, L3_conv_w1, L3_conv_w2, L3_conv_alpha, L3_conv_bn1_gamma, L3_conv_bn1_beta, L3_conv_bn1_mean, L3_conv_bn1_var, L3_conv_bn2_gamma, L3_conv_bn2_beta, L3_conv_bn2_mean, L3_conv_bn2_var):
    import jax
    import jax.numpy as jnp

    def _L0_conv_ref(x, W, pw, pb, cw, cb):
        import jax, jax.numpy as jnp
        import numpy as np
        K = 3
        PAD = 1
        GROUPS = 1
        BASES = 16

        def _conv2d(x, w, b, pad):
            out = jax.lax.conv_general_dilated(x, w, window_strides=(1, 1), padding=[(pad, pad), (pad, pad)], dimension_numbers=('NCHW', 'OIHW', 'NCHW'))
            return out + b[None, :, None, None]
        B, C, H, Wd = x.shape
        P = H * Wd
        g = GROUPS
        Og = C // g
        J = C // g * K * K
        para = _conv2d(x, pw, pb, 0)
        para = jax.nn.relu(para)
        para = _conv2d(para, cw, cb, 1)
        para = para.reshape(B, BASES, P)
        xu = jax.lax.conv_general_dilated_patches(x, filter_shape=(K, K), window_strides=(1, 1), padding=[(PAD, PAD), (PAD, PAD)])
        xu = xu.reshape(B, g, J, P)
        Wb = W.reshape(g, Og, J, BASES)
        t = jnp.einsum('goje,bgjp->bgoep', Wb, xu)
        out = jnp.einsum('bgoep,bep->bgop', t, para)
        return out.reshape(B, C, H, Wd)

    def _L1_conv_ref(x, weights, tap_offsets):
        import jax, jax.numpy as jnp
        import numpy as np
        STRIDE = 1
        PAD = 1
        EXTENT = 3

        def _bilinear_tap(xp, dy, dx, H_out, W_out):
            Hp, Wp = (xp.shape[-2], xp.shape[-1])
            y = jnp.arange(H_out, dtype=xp.dtype) * STRIDE + dy
            xc = jnp.arange(W_out, dtype=xp.dtype) * STRIDE + dx
            y0 = jnp.floor(y)
            x0 = jnp.floor(xc)
            fy = (y - y0)[None, None, :, None]
            fx = (xc - x0)[None, None, None, :]
            y0i = jnp.clip(y0.astype(jnp.int32), 0, Hp - 1)
            y1i = jnp.clip(y0.astype(jnp.int32) + 1, 0, Hp - 1)
            x0i = jnp.clip(x0.astype(jnp.int32), 0, Wp - 1)
            x1i = jnp.clip(x0.astype(jnp.int32) + 1, 0, Wp - 1)
            ry = xp[:, :, y0i, :] * (1.0 - fy) + xp[:, :, y1i, :] * fy
            return ry[:, :, :, x0i] * (1.0 - fx) + ry[:, :, :, x1i] * fx
        B, Cin, H, W = x.shape
        K = weights.shape[-1]
        xp = jnp.pad(x, ((0, 0), (0, 0), (PAD, PAD), (PAD, PAD)))
        H_out = (H + 2 * PAD - EXTENT) // STRIDE + 1
        W_out = (W + 2 * PAD - EXTENT) // STRIDE + 1
        taps = [_bilinear_tap(xp, tap_offsets[k, 0], tap_offsets[k, 1], H_out, W_out) for k in range(K)]
        g = jnp.stack(taps, 0)
        return jnp.einsum('kbiyx,oik->boyx', g, weights)

    def _L2_conv_ref(x, gk1, gk2, w1, b1, gamma1, beta1, w2, b2, gamma2, beta2):
        import jax, jax.numpy as jnp
        import numpy as np
        from jax import lax
        E, C, COUT, P, K = (4, 32, 32, 4, 16)
        B, H, W = (32, 56, 56)
        EPS = 1e-05

        def _conv(x, w, stride=1, pad=0):
            return lax.conv_general_dilated(x, w, (stride, stride), ((pad, pad), (pad, pad)), dimension_numbers=('NCHW', 'OIHW', 'NCHW'))

        def _bn(x, gamma, beta):
            mean = jnp.mean(x, axis=(0, 2, 3), keepdims=True)
            var = jnp.var(x, axis=(0, 2, 3), keepdims=True)
            xn = (x - mean) * lax.rsqrt(var + EPS)
            return gamma[None, :, None, None] * xn + beta[None, :, None, None]

        def _gate(x, k1, k2):
            g = _conv(x, k1, stride=P)
            g = _conv(g, k2)
            g = jax.nn.softmax(g, axis=1)
            b, _, h, w = g.shape
            flat = g.reshape(b, h * w)
            vals, idx = lax.top_k(flat, K)
            ret = jnp.zeros_like(flat).at[jnp.arange(b)[:, None], idx].add(vals)
            m = ret.reshape(b, 1, h, w)
            m = jnp.repeat(jnp.repeat(m, P, axis=2), P, axis=3)
            return x * m
        out = jnp.zeros_like(x)
        for e in range(E):
            g = _gate(x, gk1[e], gk2[e])
            y = _conv(g, w1[e], stride=1, pad=1) + b1[e][None, :, None, None]
            y = jax.nn.relu(_bn(y, gamma1[e], beta1[e]))
            y = _conv(y, w2[e], stride=1, pad=1) + b2[e][None, :, None, None]
            y = _bn(y, gamma2[e], beta2[e])
            y = jax.nn.relu(y + x)
            out = out + y
        return out

    def _L3_conv_ref(x, w1, w2, alpha, bn1_gamma, bn1_beta, bn1_mean, bn1_var, bn2_gamma, bn2_beta, bn2_mean, bn2_var):
        import jax, jax.numpy as jnp
        import numpy as np
        EPS = 1e-05

        def _conv3x3(x, w):
            return jax.lax.conv_general_dilated(x, w, window_strides=(1, 1), padding=((1, 1), (1, 1)), dimension_numbers=('NCHW', 'OIHW', 'NCHW'))

        def _bn(x, gamma, beta, mean, var):
            inv = gamma / jnp.sqrt(var + EPS)
            return x * inv[None, :, None, None] + (beta - mean * inv)[None, :, None, None]
        w1_eff = jnp.einsum('e,eoihw->oihw', alpha, w1)
        w2_eff = jnp.einsum('e,eoihw->oihw', alpha, w2)
        out = _conv3x3(x, w1_eff)
        out = jax.nn.relu(_bn(out, bn1_gamma, bn1_beta, bn1_mean, bn1_var))
        out = _conv3x3(out, w2_eff)
        out = _bn(out, bn2_gamma, bn2_beta, bn2_mean, bn2_var)
        return jax.nn.relu(out + x)

    def _gn(v, G=32, eps=1e-05):
        B_, C_, H_, W_ = v.shape
        g = v.reshape(B_, G, C_ // G, H_, W_)
        m = jnp.mean(g, axis=(2, 3, 4), keepdims=True)
        s = jnp.var(g, axis=(2, 3, 4), keepdims=True)
        return ((g - m) / jnp.sqrt(s + eps)).reshape(v.shape)

    def _ln_c(v, eps=1e-06):
        m = jnp.mean(v, axis=1, keepdims=True)
        s = jnp.var(v, axis=1, keepdims=True)
        return (v - m) / jnp.sqrt(s + eps)

    def _ln_t(v, eps=1e-05):
        m = jnp.mean(v, axis=-1, keepdims=True)
        s = jnp.var(v, axis=-1, keepdims=True)
        return (v - m) / jnp.sqrt(s + eps)

    def _to_tokens(v):
        B_, C_, H_, W_ = v.shape
        return v.reshape(B_, C_, H_ * W_).transpose(0, 2, 1)

    def _from_tokens(t, like):
        B_, C_, H_, W_ = like.shape
        return t.transpose(0, 2, 1).reshape(B_, C_, H_, W_)
    x = x + _L0_conv_ref(_gn(x), L0_conv_W, L0_conv_pw, L0_conv_pb, L0_conv_cw, L0_conv_cb)
    x = x + _L1_conv_ref(_gn(x), L1_conv_weights, L1_conv_tap_offsets)
    x = x + _L2_conv_ref(_gn(x), L2_conv_gk1, L2_conv_gk2, L2_conv_w1, L2_conv_b1, L2_conv_gamma1, L2_conv_beta1, L2_conv_w2, L2_conv_b2, L2_conv_gamma2, L2_conv_beta2)
    x = x + _L3_conv_ref(_gn(x), L3_conv_w1, L3_conv_w2, L3_conv_alpha, L3_conv_bn1_gamma, L3_conv_bn1_beta, L3_conv_bn1_mean, L3_conv_bn1_var, L3_conv_bn2_gamma, L3_conv_bn2_beta, L3_conv_bn2_mean, L3_conv_bn2_var)
    return x

_drawn_inputs = setup_inputs


def setup_inputs(seed=0):
    import zlib

    import numpy as np

    out = dict(_drawn_inputs(seed))
    spreads = {'L0_conv_pb': (0.0, 0.1),
     'L0_conv_cb': (0.0, 0.1),
     'L2_conv_gamma1': (1.0, 0.2),
     'L2_conv_beta1': (0.0, 0.756),
     'L2_conv_gamma2': (1.0, 0.2),
     'L2_conv_beta2': (0.0, 0.275),
     'L3_conv_bn1_gamma': (1.0, 0.2),
     'L3_conv_bn1_beta': (0.0, 0.419),
     'L3_conv_bn1_mean': (0.0, 0.452),
     'L3_conv_bn2_gamma': (1.0, 0.2),
     'L3_conv_bn2_beta': (0.0, 0.714),
     'L3_conv_bn2_mean': (0.0, 0.682)}
    factors = {'L2_conv_b1': 8.0, 'L2_conv_b2': 8.0}
    for name, (base, spread) in spreads.items():
        noise = np.random.default_rng([zlib.crc32(name.encode()), seed]).standard_normal(out[name].shape)
        drawn = base * np.exp(spread * noise) if base else spread * noise
        out[name] = jnp.asarray(drawn.astype(out[name].dtype))
    for name, factor in factors.items():
        out[name] = (out[name] * factor).astype(out[name].dtype)
    return out
```

```python
from contextlib import ExitStack

import concourse.bass as bass
from concourse import mybir

F32 = mybir.dt.float32
F32R = mybir.dt.float32r
ALU = mybir.AluOpType
ACT = mybir.ActivationFunctionType
AX = mybir.AxisListType

B, C, H, W = 4, 32, 64, 64
P = B * C
PIX = H * W
E0 = 16
NE = 4
NM = 10
TAPS = 9
PW = W + 2
PH = 68
CH = 512
NCH = PIX // CH
CR = CH // W
EPS = 1e-5
SPAN = 2 * PW + 2
S0 = CH + SPAN - 2
TAIL = H * PW - NCH * CH
R1 = 2 * CR + 3
CROWS = 8
REP = H - CROWS + 1
QI = CROWS + 2
NPIX = B * PIX

PB, CB, B1, G1, BE1, B2, G2, BE2 = 0, 1, 2, 3, 4, 5, 9, 13
N1G, N1B, N1M, N1V, N2G, N2B, N2M, N2V, AL, DY, DX = 17, 18, 19, 20, 21, 22, 23, 24, 25, 35, 44
NPAR = 53


def build(nc, x, w0, pw, cw, w1, w2a, w2b, w3a, w3b, par, out):
    ctx = ExitStack()
    with ctx:
        cursor = [nc.sbuf_base]

        def sb(name, shape, dt=F32, at=None):
            size = 4
            for n in shape[1:]:
                size *= n
            size = -(-size // 32) * 32
            if at is None:
                at = -(-cursor[0] // 32) * 32
                cursor[0] = at + size
            return nc.alloc_sbuf_tensor_at(name, shape, dt, offset=at), at, at + size

        def sem(name):
            return ctx.enter_context(nc.semaphore(name))

        X = sb("X", [P, PIX])[0]
        U = sb("U", [P, PIX])[0]
        IMG = sb("IMG", [P, PH * PW])[0]
        PAR = sb("PAR", [P, NPAR])[0]
        ST = sb("ST", [P, NCH, 6])[0]
        MV = sb("MV", [P, 2])[0]
        VE = sb("VE", [P, 1])[0]
        RS = sb("RS", [P, 1])[0]
        NMR = sb("NMR", [P, 1])[0]
        MHALF = sb("MHALF", [P, 4])[0]
        WE = sb("WE", [P, 4, C])[0]
        W1R = sb("W1R", [P, C, TAPS])[0]
        CO = sb("CO", [P, 4, TAPS])[0]
        CX = sb("CX", [P, TAPS])[0]
        XG = sb("XG", [P, 1])[0]
        CT = sb("CT", [P, TAPS])[0]
        WT = sb("WT", [P, C, TAPS])[0]
        W2A = sb("W2A", [96, 3, NE * C])[0]
        W2B = sb("W2B", [96, NE, 3, C])[0]
        W3A = sb("W3A", [96, 3 * C])[0]
        W3B = sb("W3B", [96, 3 * C])[0]
        AVG = sb("AVG", [P, B, C])[0]
        CI = sb("CI", [P, 7 * PW + 4])[0]
        ID = sb("ID", [P, P])[0]
        S3 = sb("S3", [P, 8])[0]
        top = cursor[0]
        HI, a, b_ = sb("HI", [P, PH * PW], F32R)
        LO = sb("LO", [P, PH * PW], F32R)[0]
        P1 = sb("P1", [P, PH * PW])[0]
        HS = [sb(f"HS{i}", [P, B, S0], F32R)[0] for i in range(2)]
        LS = [sb(f"LS{i}", [P, B, S0], F32R)[0] for i in range(2)]
        WA = sb("WA", [P, 3, CH], F32R)[0]
        WB = sb("WB", [96, 3, CH], F32R)[0]
        WC = sb("WC", [P, 2, CH], F32R)[0]
        RA, ra_at, _ = sb("RA", [P, 3, CH])
        RC = sb("RC", [P, 2, CH])[0]
        PWB = sb("PWB", [P, 2, B, E0])[0]
        CWB = sb("CWB", [P, 6, B, E0])[0]
        PARA = sb("PARA", [P, 5, CH])[0]
        PT = sb("PT", [P, 4 * CH + 64], at=ra_at)[0]
        PROD = [sb(f"PROD{i}", [P, CH])[0] for i in range(2)]
        RED = [sb(f"RED{i}", [P, P])[0] for i in range(2)]
        WR3 = sb("WR3", [96, NM, 3 * C])[0]
        WR3B = sb("WR3B", [96, NM, 3 * C])[0]
        assert cursor[0] <= nc.sbuf_usable_end, (cursor[0], nc.sbuf_usable_end)
        hi_end = cursor[0]
        cursor[0] = top
        SK = [sb(f"SK{i}", [P, B, R1 * PW])[0] for i in range(2)]
        H1 = sb("H1", [P, B * QI * PW + 4])[0]
        SH = sb("SH", [P, NE, B * QI * PW])[0]
        CS = sb("CS", [96, B, 7 * PW])[0]
        Z = sb("Z", [P, NE, CH])[0]
        T2 = [sb(f"T2{i}", [P, CH])[0] for i in range(4)]
        IMG2 = sb("IMG2", [P, PH * PW])[0]
        S1 = sb("S1", [P, 5, 6])[0]
        S2 = sb("S2", [P, NE, 3, 6])[0]
        M2 = sb("M2", [P, NE, 2])[0]
        Q2 = sb("Q2", [P, 8, NE])[0]
        NA = sb("NA", [P, NE, 3])[0]
        AS = sb("AS", [P, 3])[0]
        OT = [sb(f"OT{i}", [P, CH])[0] for i in range(4)]
        assert cursor[0] <= hi_end

        ps = [ctx.enter_context(nc.psum_tensor(f"ps{i}", [P, CH], F32)) for i in range(8)]

        x_in = [sem(f"x_in{i}") for i in range(4)]
        w_pw, w_cw, w_main, w_par, w_l1, w_l2, w_l3 = (sem(f"w_{n}") for n in ("pw", "cw", "main", "par", "l1", "l2", "l3"))
        zeroed = sem("zeroed")
        wsplit = sem("wsplit")
        wl1_ready = sem("wl1_ready")
        wl3_ready = sem("wl3_ready")
        pstep = sem("pstep")
        vstep = sem("vstep")
        var_ready = sem("var_ready")
        rstd_ready = sem("rstd_ready")
        coef_ready = sem("coef_ready")
        u0_done = sem("u0_done")
        hi_done = sem("hi_done")
        lo_done = sem("lo_done")
        pw_done = sem("pw_done")
        p1_done = sem("p1_done")
        para_done = sem("para_done")
        para_sb = sem("para_sb")
        pt_done = sem("pt_done")
        pt_sb = sem("pt_sb")
        strip0 = [sem(f"strip0_{i}") for i in range(2)]
        t_done = sem("t_done")
        mult_done = sem("mult_done")
        red_done = sem("red_done")
        tr_done = sem("tr_done")
        x1_done = sem("x1_done")
        img_v = sem("img_v")
        img_a = sem("img_a")
        strip1 = [sem(f"strip1_{i}") for i in range(2)]
        c1_done = sem("c1_done")
        x2_done = sem("x2_done")
        ci_done = sem("ci_done")
        u2_done = sem("u2_done")
        cs_ready = sem("cs_ready")
        k1_done = sem("k1_done")
        sh1_ready = sem("sh1_ready")
        h1_done = sem("h1_done")
        sh_ready = sem("sh_ready")
        k2_done = sem("k2_done")
        bm_ready = sem("bm_ready")
        bm_done = sem("bm_done")
        sh2_ready = sem("sh2_ready")
        z_done = sem("z_done")
        as_ready = sem("as_ready")
        xa_done = sem("xa_done")
        strip3 = [sem(f"strip3_{i}") for i in range(2)]
        c3_done = sem("c3_done")
        g_done = sem("g_done")
        strip4 = [sem(f"strip4_{i}") for i in range(2)]
        c4_done = sem("c4_done")
        t4_done = sem("t4_done")
        r4_done = sem("r4_done")
        o_done = sem("o_done")
        x3_done = sem("x3_done")
        out_done = [sem(f"out_done{i}") for i in range(4)]
        nmr_done = sem("nmr_done")
        st_done = sem("st_done")
        sh_avg = sem("sh_avg")
        d_done = sem("d_done")

        def rows(ap, r, n, c=1, w=W):
            return ap[:, r * PW:(r + n) * PW].rearrange("p (r c) -> p r c", c=PW)[:, :, c:c + w]

        block = ctx.enter_context(nc.Block())

        @block.sync
        def _(sp):
            for i in range(4):
                sp.dma_start(X[:, i * 1024:(i + 1) * 1024], x[:, i * 1024:(i + 1) * 1024]).then_inc(x_in[i], 16)
            sp.dma_start(PAR[:, :], par).then_inc(w_par, 16)
            for g in range(3):
                sp.dma_start(RA[32 * g:32 * g + 32, :, :], w0[g:9:3, :, :].rearrange("t c n -> c t n")).then_inc(w_main, 16)
            sp.dma_start(RA[96:128, :, :], w0[0:9:3, :, :].rearrange("t c n -> c t n")).then_inc(w_main, 16)
            for g, tap in enumerate((1, 2, 4, 5)):
                sp.dma_start(RC[32 * g:32 * g + 32, 0, :], w0[tap, :, :]).then_inc(w_main, 16)
            for g, tap in enumerate((7, 8)):
                sp.dma_start(RC[32 * g:32 * g + 32, 1, :], w0[tap, :, :]).then_inc(w_main, 16)
            sp.dma_start(W2A[:, :, :], w2a).then_inc(w_l2, 16)
            sp.dma_start(W2B[:, :, :, :], w2b).then_inc(w_l2, 16)
            sp.dma_start(WR3[:, :, :], w3a).then_inc(w_l3, 16)
            sp.dma_start(WR3B[:, :, :], w3b).then_inc(w_l3, 16)
            for g in range(4):
                sp.dma_start(W1R[32 * g:32 * g + 32, :, :], w1).then_inc(w_l1, 16)

            def strip_block0(s, half, n):
                for b in range(B):
                    pb = slice(32 * b, 32 * b + 32)
                    hs, ls = HS[half], LS[half]
                    copies = [(hs, g, HI, g, n + 2 * PW) for g in range(3)] + [(hs, 3, LO, 0, n + 2 * PW)]
                    copies += [(ls, g, LO, off, n + 2 * PW if g < 2 else n) for g, off in enumerate((1, 2, PW + 1, PW + 2))]
                    for dst, g, src, off, m in copies:
                        sp.dma_start(dst[32 * g:32 * g + 32, b, 0:m].bitcast(F32),
                                     src[pb, bass.ds(s * CH + off, m)].bitcast(F32)).then_inc(strip0[half], 16)

            for half in range(2):
                sp.wait_ge(lo_done, half + 2)
                strip_block0(half, half, CH)
            sp.wait_ge(lo_done, NCH)
            with sp.Fori(1, 4) as it:
                for half in range(2):
                    sp.wait_ge(t_done, 32 * it - 16 + 16 * half)
                    strip_block0(2 * it + half, half, CH)
            sp.wait_ge(t_done, 16 * 7)
            strip_block0(NCH, 0, TAIL)

            def strips(stack, ready, img, groups, n_rows, need, free):
                for s in range(4):
                    need(s)
                    if s >= 2:
                        free(s)
                    for b in range(B):
                        for g in range(groups):
                            a = 2 * s * CR * PW + g
                            sp.dma_start(stack[s % 2][32 * g:32 * g + 32, b, 0:n_rows * PW], img[32 * b:32 * b + 32, a:a + n_rows * PW]).then_inc(ready[s % 2], 16)

            def need_img(base):
                def need(s):
                    last = min(2 * s + 2, NCH - 1)
                    sp.wait_ge(img_v, 4 * base + last // 2 + 1)
                    sp.wait_ge(img_a, 4 * base + (last + 1) // 2)
                return need

            strips(SK, strip1, IMG, 4, R1, need_img(0), lambda s: sp.wait_ge(c1_done, 2 * (s - 1)))
            sp.wait_ge(ci_done, 1)
            for b in range(B):
                for g in range(3):
                    sp.dma_start(CS[32 * g:32 * g + 32, b, :], CI[32 * b:32 * b + 32, g:g + 7 * PW]).then_inc(cs_ready, 16)
            sp.wait_ge(h1_done, 5)
            for e in range(NE):
                for g in range(3):
                    sp.dma_start(SH[32 * g:32 * g + 32, e, :], H1[32 * e:32 * e + 32, g:g + B * QI * PW]).then_inc(sh_ready, 16)
            strips(SK, strip3, IMG, 3, R1 - 1, need_img(1), lambda s: sp.wait_ge(c3_done, 2 * (s - 1)))

            def need4(s):
                sp.wait_ge(g_done, min(2 * s + 3, NCH))
                if s == 0:
                    sp.wait_ge(c3_done, NCH - 2)
                if s == 1:
                    sp.wait_ge(c3_done, NCH)
            strips(SK, strip4, IMG2, 3, R1 - 1, need4, lambda s: sp.wait_ge(c4_done, 2 * (s - 1)))
            for k in range(NCH):
                sp.wait_ge(o_done, k + 1)
                sp.dma_start(out[:, k * CH:(k + 1) * CH], OT[k % 4][:, :]).then_inc(out_done[k % 4], 16)
            for i in range(4):
                sp.wait_ge(out_done[i], 16 * NCH // 4)

        @block.gpsimd
        def _(gp):
            n = [0]

            def step(ins):
                n[0] += 1
                ins.then_inc(pstep, 1)
                gp.wait_ge(pstep, n[0])

            gp.memset(PWB[:, :, :, :], 0.0).then_inc(zeroed, 1)
            gp.memset(CWB[:, :, :, :], 0.0).then_inc(zeroed, 1)
            gp.memset(P1[:, :], 0.0).then_inc(zeroed, 1)
            for m in (HI, LO, IMG):
                gp.memset(m[:, 0:PW + 1].bitcast(F32), 0.0).then_inc(zeroed, 1)
                gp.memset(m[:, PW + W + 1:(H + 1) * PW + W + 1].bitcast(F32).rearrange("p (r c) -> p r c", c=PW)[:, :, 0:PW - W], 0.0).then_inc(zeroed, 1)
                gp.memset(m[:, (H + 1) * PW + 1:PH * PW].bitcast(F32), 0.0).then_inc(zeroed, 1)
            gp.memset(MHALF[:, :], -0.5).then_inc(zeroed, 1)
            step(gp.memset(ID[:, :], 0.0))
            step(gp.affine_select(out=ID[:, :], in_=ID[:, :], compare_op=ALU.not_equal, fill=1.0, base=0,
                                  pattern=[[-1, P]], channel_multiplier=1))
            gp.memset(CI[:, :], 0.0).then_inc(zeroed, 1)

            def rstd(k):
                gp.wait_ge(var_ready, k)
                gp.tensor_tensor(RS[:, :], VE[:, :], MHALF[:, 0:1], ALU.pow).then_inc(rstd_ready, 1)

            rstd(1)
            for k in range(NCH):
                gp.wait_ge(hi_done, k + 1)
                gp.tensor_tensor(rows(LO, 1 + k * CR, CR), U[:, k * CH:(k + 1) * CH].rearrange("p (r c) -> p r c", c=W),
                                 rows(HI, 1 + k * CR, CR).bitcast(F32), ALU.subtract).then_inc(lo_done, 1)

            step(gp.memset(AVG[:, :, :], 0.0))
            for b in range(B):
                step(gp.affine_select(out=AVG[:, :, :], in_=AVG[:, :, :], compare_op=ALU.not_equal, fill=1.0 / B,
                                      base=-32 * b, pattern=[[0, B], [-1, C]], channel_multiplier=1))
            gp.wait_ge(w_par, 16)
            for g in range(4):
                step(gp.memset(XG[32 * g:32 * g + 32, :], float(g)))

            step(gp.tensor_scalar(CX[:, :], PAR[:, DX:DX + TAPS], XG[:, 0:1], None, ALU.subtract))
            step(gp.tensor_scalar(CT[:, :], CX[:, :], -1.0, 1.0, ALU.mult, ALU.add))
            step(gp.tensor_scalar(CX[:, :], CX[:, :], 1.0, 1.0, ALU.mult, ALU.add))
            step(gp.tensor_tensor(CT[:, :], CT[:, :], CX[:, :], ALU.subtract))
            step(gp.tensor_scalar(CT[:, :], CT[:, :], 0.0, None, ALU.min))
            step(gp.tensor_tensor(CX[:, :], CX[:, :], CT[:, :], ALU.add))
            step(gp.tensor_scalar(CX[:, :], CX[:, :], 0.0, None, ALU.max))
            for y in range(4):
                cy = CO[:, y, :]
                step(gp.tensor_scalar(CT[:, :], PAR[:, DY:DY + TAPS], -1.0, 1.0 + y, ALU.mult, ALU.add))
                step(gp.tensor_scalar(cy, PAR[:, DY:DY + TAPS], 1.0, 1.0 - y, ALU.mult, ALU.add))
                step(gp.tensor_tensor(CT[:, :], CT[:, :], cy, ALU.subtract))
                step(gp.tensor_scalar(CT[:, :], CT[:, :], 0.0, None, ALU.min))
                step(gp.tensor_tensor(cy, cy, CT[:, :], ALU.add))
                step(gp.tensor_scalar(cy, cy, 0.0, None, ALU.max))
                step(gp.tensor_tensor(cy, cy, CX[:, :], ALU.mult))
            gp.wait_ge(w_l1, 64)
            for y in range(4):
                step(gp.tensor_tensor(WT[:, :, :], W1R[:, :, :], CO[:, y:y + 1, :].broadcast_to([P, C, TAPS]), ALU.mult))
                for k in range(1, TAPS):
                    ins = gp.tensor_tensor(WT[:, :, 0] if k < TAPS - 1 else WE[:, y, :], WT[:, :, 0], WT[:, :, k], ALU.add)
                    step(ins)
            gp.memset(MHALF[:, 1:2], 1.0).then_inc(wl1_ready, 1)
            gp.wait_ge(w_l3, 32)
            for raw, eff in ((WR3, W3A), (WR3B, W3B)):
                step(gp.tensor_scalar(eff[:, :], raw[:, 0, :], PAR[0:96, AL:AL + 1], None, ALU.mult))
                for e in range(1, NM):
                    step(gp.tensor_scalar(raw[:, e, :], raw[:, e, :], PAR[0:96, AL + e:AL + e + 1], None, ALU.mult))
                    step(gp.tensor_tensor(eff[:, :], eff[:, :], raw[:, e, :], ALU.add))
            for i, (g, be, m, v) in enumerate(((N1G, N1B, N1M, N1V), (N2G, N2B, N2M, N2V))):
                sc, sh = S3[:, 2 * i:2 * i + 1], S3[:, 2 * i + 1:2 * i + 2]
                step(gp.tensor_scalar(sc, PAR[:, v:v + 1], 1.0, EPS, ALU.mult, ALU.add))
                step(gp.tensor_tensor(sc, sc, MHALF[:, 0:1], ALU.pow))
                step(gp.tensor_tensor(sc, sc, PAR[:, g:g + 1], ALU.mult))
                step(gp.tensor_tensor(sh, PAR[:, m:m + 1], sc, ALU.mult))
                step(gp.tensor_tensor(sh, PAR[:, be:be + 1], sh, ALU.subtract))
            gp.memset(MHALF[:, 2:3], 1.0).then_inc(wl3_ready, 1)
            rstd(2)
            gp.memset(H1[:, :], 0.0).then_inc(zeroed, 1)
            gp.memset(IMG2[:, :], 0.0).then_inc(zeroed, 1)
            rstd(3)

            gp.wait_ge(bm_ready, 1)
            gp.tensor_tensor(Q2[:, 7, 1:2], Q2[:, 7, 0:1], MHALF[:, 0:1], ALU.pow).then_inc(bm_done, 1)
            gp.wait_ge(bm_ready, 4)
            for e in range(NE):
                ins = gp.tensor_tensor(Q2[:, 4, e:e + 1], Q2[:, 3, e:e + 1], MHALF[:, 0:1], ALU.pow)
            ins.then_inc(bm_done, 1)
            rstd(4)
            for k in range(NCH):
                gp.wait_ge(r4_done, k + 1)
                if k >= 4:
                    gp.wait_ge(out_done[k % 4], 16 * (k // 4))
                gp.tensor_tensor(OT[k % 4][:, :], T2[k % 4][:, :], X[:, k * CH:(k + 1) * CH], ALU.add).then_inc(o_done, 1)

        @block.scalar
        def _(act):
            act.wait_ge(zeroed, 2)
            for b in range(B):
                act.dma_start(PWB[32 * b:32 * b + 32, :, b, :], pw).then_inc(w_pw, 16)
            for b in range(B):
                act.dma_start(CWB[16 * b:16 * b + 16, 0:3, b, :], cw[:, 0, :, :]).then_inc(w_cw, 16)
                act.dma_start(CWB[64 + 16 * b:80 + 16 * b, 0:3, b, :], cw[:, 1, :, :]).then_inc(w_cw, 16)
                act.dma_start(CWB[16 * b:16 * b + 16, 3:6, b, :], cw[:, 2, :, :]).then_inc(w_cw, 16)
            act.wait_ge(zeroed, 13)
            for k in range(NCH):
                act.wait_ge(u0_done, k + 1)
                act.activation(rows(HI, 1 + k * CR, CR), U[:, k * CH:(k + 1) * CH].rearrange("p (r c) -> p r c", c=W), ACT.Copy).then_inc(hi_done, 1)
            for k in range(NCH):
                act.wait_ge(pw_done, k + 1)
                if k == 0:
                    act.wait_ge(w_par, 16)
                src = ps[6 + k % 2]
                for d in range(2):
                    p = slice(64 * d, 64 * d + 64)
                    act.activation(rows(P1[p, :], 1 - d + k * CR, CR), src[p, :].rearrange("p (r c) -> p r c", c=W), ACT.Relu,
                                   bias=PAR[p, PB:PB + 1]).then_inc(p1_done, 1)
            for q in range(4):
                act.wait_ge(para_done, q + 1)
                act.activation(PARA[:, q, :], ps[4 + q % 2][:, :], ACT.Identity, bias=PAR[:, CB:CB + 1]).then_inc(para_sb, 1)
            act.wait_ge(para_done, 5)
            act.activation(PARA[0:64, 4, 0:TAIL], ps[4][0:64, 0:TAIL], ACT.Identity, bias=PAR[0:64, CB:CB + 1]).then_inc(para_sb, 1)
            with act.Fori(0, 4) as it:
                for half in range(2):
                    act.wait_ge(tr_done, 8 * it + 4 * half + 4)
                    act.activation(P1[:, bass.ds(it * 2 * CH + half * CH, CH)], ps[4 + half][:, :], ACT.Copy).then_inc(d_done, 1)
            act.wait_ge(tr_done, 33)
            act.activation(P1[:, NCH * CH:NCH * CH + TAIL], ps[4][:, 0:TAIL], ACT.Copy).then_inc(d_done, 1)

            def normalise(base):
                act.wait_ge(coef_ready, base + 1)
                for k in range(1, NCH, 2):
                    act.activation(rows(IMG, 1 + k * CR, CR), X[:, k * CH:(k + 1) * CH].rearrange("p (r c) -> p r c", c=W), ACT.Identity,
                                   bias=NMR[:, 0:1], scale=RS[:, 0:1]).then_inc(img_a, 1)

            normalise(0)
            act.wait_ge(coef_ready, 2)
            act.activation(U[:, :], X[:, :], ACT.Identity, bias=NMR[:, 0:1], scale=RS[:, 0:1]).then_inc(u2_done, 1)
            act.wait_ge(sh1_ready, 1)
            act.wait_ge(zeroed, 16)
            h4 = H1[:, 0:B * QI * PW].rearrange("p (b r c) -> p b r c", b=B, c=PW)
            for r in range(3):
                ins = act.activation(h4[:, :, 6 + r, 1:1 + W], h4[:, :, 6 + r, 1:1 + W], ACT.Relu, bias=Q2[:, 7, 3:4])
            ins.then_inc(h1_done, 1)
            for b in range(B):
                act.activation(h4[:, b, 1:6, 1:1 + W], ps[b][:, 0:5 * W].rearrange("p (r c) -> p r c", c=W), ACT.Relu,
                               bias=Q2[:, 7, 3:4], scale=Q2[:, 7, 2:3]).then_inc(h1_done, 1)
            act.wait_ge(sh2_ready, 1)
            for e in range(NE):
                act.activation(Z[:, e, :], ps[e][:, :], ACT.Identity, bias=Q2[:, 6, e:e + 1], scale=Q2[:, 5, e:e + 1]).then_inc(z_done, 1)
            act.wait_ge(as_ready, 1)
            xin = X[:, 6 * W:(H - 1) * W].rearrange("p (r c) -> p r c", c=W)
            act.activation(xin[:, :, 1:W - 1], xin[:, :, 1:W - 1], ACT.Identity, bias=AS[:, 1:2]).then_inc(xa_done, 1)
            act.activation(xin[:, :, 0:1], xin[:, :, 0:1], ACT.Identity, bias=AS[:, 0:1]).then_inc(xa_done, 1)
            act.activation(xin[:, :, W - 1:W], xin[:, :, W - 1:W], ACT.Identity, bias=AS[:, 2:3]).then_inc(xa_done, 1)
            act.wait_ge(coef_ready, 3)
            for k in range(1, NCH, 2):
                act.activation(rows(IMG, 1 + k * CR, CR), X[:, k * CH:(k + 1) * CH].rearrange("p (r c) -> p r c", c=W), ACT.Identity,
                               bias=NMR[:, 0:1], scale=RS[:, 0:1]).then_inc(img_a, 1)
            act.wait_ge(wl3_ready, 1)
            for k in range(NCH):
                act.wait_ge(c3_done, k + 1)
                act.activation(rows(IMG2, 1 + k * CR, CR), ps[k % 4][:, :].rearrange("p (r c) -> p r c", c=W), ACT.Relu,
                               bias=S3[:, 1:2], scale=S3[:, 0:1]).then_inc(g_done, 1)
            for k in range(NCH):
                act.wait_ge(t4_done, k + 1)
                act.activation(T2[k % 4][:, :], T2[k % 4][:, :], ACT.Relu, bias=S3[:, 3:4]).then_inc(r4_done, 1)

        @block.tensor
        def _(pe):
            pe.wait_ge(w_pw, 64)
            for k in range(NCH):
                pe.wait_ge(u0_done, k + 1)
                if k >= 2:
                    pe.wait_ge(p1_done, 2 * (k - 1))
                pe.matmul(ps[6 + k % 2][:, :], PWB[:, :, :, :], U[:, k * CH:(k + 1) * CH], start=True, stop=True).then_inc(pw_done, 1)
            pe.wait_ge(w_cw, 192)
            for q in range(5):
                pe.wait_ge(p1_done, min(4 * q + 6, 16))
                if q >= 2:
                    pe.wait_ge(para_sb, q - 1)
                n = CH if q < 4 else TAIL
                for i in range(6):
                    for h in range(2 if q < 4 else 1):
                        a = (2 * q + h) * CH + i % 3 + (0 if i < 3 else 2 * PW)
                        ins = pe.matmul(ps[4 + q % 2][64 * h:64 * h + 64, 0:n], CWB[:, i, :, :], P1[:, a:a + n],
                                        start=(i == 0), stop=(i == 5))
                ins.then_inc(para_done, 1)
            for q in range(5):
                pe.wait_ge(para_sb, q + 1)
                if q >= 2:
                    pe.wait_ge(pt_sb, q - 1)
                k = P if q < 4 else 64
                for t in range(4 if q < 4 else 1):
                    ins = pe.transpose(ps[6 + q % 2][:, t * P:t * P + k], PARA[0:k, q, t * P:(t + 1) * P], ID[0:k, 0:k])
                ins.then_inc(pt_done, 1)

            def tile(half, t, b):
                px = lambda s, off, k=P: s[half][0:k, b, off + t * P:off + (t + 1) * P]
                for dy in range(3):
                    pe.matmul(ps[b][:, :], px(HS, dy * PW), WA[:, dy, :], start=(dy == 0), stop=False)
                    pe.matmul(ps[b][:, :], px(HS, dy * PW, 96), WB[:, dy, :], start=False, stop=False)
                pe.matmul(ps[b][:, :], px(LS, 0), WC[:, 0, :], start=False, stop=False)
                pe.matmul(ps[b][:, :], px(LS, 2 * PW, 64), WC[0:64, 1, :], start=False, stop=True).then_inc(t_done, 1)

            def back(half, t, g, strip, first=False):
                pe.wait_ge(red_done, 4 * g + 4)
                if t == 0 and not first:
                    pe.wait_ge(d_done, strip - 1)
                pe.transpose(ps[4 + half][:, t * P:(t + 1) * P], RED[t % 2][:, :], ID[:, :]).then_inc(tr_done, 1)

            def block0(it, first):
                for half in range(2):
                    pe.wait_ge(strip0[half], 16 * 32 * (it + 1))
                    for t in range(4):
                        g = it * 8 + 4 * half + t
                        for b in range(B):
                            if not (first and 4 * half + t == 0):
                                pe.wait_ge(mult_done, 4 * g + b - 3)
                            tile(half, t, b)
                        if t > 0:
                            back(half, t - 1, g - 1, 2 * it + half, first)
                        elif not (first and half == 0):
                            back(1 - half, 3, g - 1, 0)

            pe.wait_ge(wsplit, 3)
            block0(0, True)
            with pe.Fori(1, 4) as it:
                block0(it, False)
            pe.wait_ge(strip0[0], 16 * 32 * 5)
            for b in range(B):
                pe.wait_ge(mult_done, 4 * 32 + b - 3)
                tile(0, 0, b)
            back(1, 3, 31, 7)
            back(0, 0, 32, 8)

            def conv(stack, ready, wt, groups, slots, done, free):
                for s in range(4):
                    pe.wait_ge(ready[s % 2], 16 * B * groups * (s // 2 + 1))
                    for cc in range(2):
                        k = 2 * s + cc
                        if k >= 4:
                            free(k)
                        for y in range(slots):
                            for b in range(B):
                                ins = pe.matmul(ps[k % 4][32 * b:32 * b + 32, :], wt(y), rows(stack[s % 2][0:32 * groups, b, :], cc * CR + y, CR, 0),
                                                start=(y == 0), stop=(y == slots - 1))
                        ins.then_inc(done, 1)

            pe.wait_ge(wl1_ready, 1)
            conv(SK, strip1, lambda y: WE[:, y, :], 4, 4, c1_done, lambda k: pe.wait_ge(x2_done, k - 3))
            pe.wait_ge(w_l2, 32)
            pe.wait_ge(cs_ready, 16 * 12)
            pe.wait_ge(x2_done, NCH)
            for b in range(B):
                for dy in range(3):
                    ins = pe.matmul(ps[b][:, 0:5 * W], W2A[:, dy, :], rows(CS[:, b, :], dy, 5, 0), start=(dy == 0), stop=(dy == 2))
                ins.then_inc(k1_done, 1)
            pe.wait_ge(sh_ready, 16 * 12)
            for e in range(NE):
                for dy in range(3):
                    for b in range(B):
                        a = b * QI * PW
                        ins = pe.matmul(ps[e][32 * b:32 * b + 32, :], W2B[:, e, dy, :], rows(SH[0:96, e, a:a + QI * PW], dy, CROWS, 0),
                                        start=(dy == 0), stop=(dy == 2))
                ins.then_inc(k2_done, 1)
            for i, q in ((0, 0), (1, 2)):
                pe.wait_ge(bm_ready, 2 + i)
                pe.matmul(ps[4][:, 8 * i:8 * i + NE], AVG[:, :, :], Q2[:, q, :], start=True, stop=True).then_inc(sh_avg, 1)
            pe.wait_ge(wl3_ready, 1)
            pe.wait_ge(z_done, NE)
            conv(SK, strip3, lambda y: W3A[:, 32 * y:32 * y + 32], 3, 3, c3_done, lambda k: pe.wait_ge(g_done, k - 3))
            pe.wait_ge(g_done, NCH)
            conv(SK, strip4, lambda y: W3B[:, 32 * y:32 * y + 32], 3, 3, c4_done, lambda k: pe.wait_ge(t4_done, k - 3))

        @block.vector
        def _(ve):
            n = [0]

            def step(ins):
                n[0] += 1
                ins.then_inc(vstep, 1)
                ve.wait_ge(vstep, n[0])

            def coefs(k):
                step(ve.bn_aggr(MV[:, :], ST[:, :, :]))
                ve.tensor_scalar(VE[:, :], MV[:, 1:2], EPS, None, ALU.add).then_inc(var_ready, 1)
                ve.wait_ge(rstd_ready, k)
                ve.scalar_tensor_tensor(NMR[:, :], MV[:, 0:1], -1.0, RS[:, :], ALU.mult, ALU.mult).then_inc(nmr_done, 1)

            for k in range(NCH):
                if k % 2 == 0:
                    ve.wait_ge(x_in[k // 2], 16)
                ins = ve.bn_stats(ST[:, k, :], X[:, k * CH:(k + 1) * CH])
            step(ins)
            coefs(1)
            for k in range(NCH):
                ve.tensor_scalar(U[:, k * CH:(k + 1) * CH], X[:, k * CH:(k + 1) * CH], MV[:, 0:1], RS[:, 0:1], ALU.subtract, ALU.mult).then_inc(u0_done, 1)
            ve.wait_ge(w_main, 160)
            ve.tensor_copy(WA[:, :, :], RA[:, :, :]).then_inc(wsplit, 1)
            ve.tensor_copy(WC[:, 0, :], RC[:, 0, :])
            ve.tensor_copy(WC[0:64, 1, :], RC[0:64, 1, :]).then_inc(wsplit, 1)
            ve.wait_ge(wsplit, 2)
            ve.tensor_tensor(WB[:, :, :], RA[0:96, :, :], WA[0:96, :, :].bitcast(F32), ALU.subtract).then_inc(wsplit, 1)
            ve.wait_ge(wsplit, 3)
            for q in range(5):
                ve.wait_ge(pt_done, q + 1)
                n_pt = CH if q < 4 else 64
                ve.tensor_copy(PT[:, q * CH:q * CH + n_pt], ps[6 + q % 2][:, 0:n_pt]).then_inc(pt_sb, 1)
            ve.wait_ge(pt_sb, 5)

            def reduce(half, t, b, m):
                ve.wait_ge(mult_done, m + 1)
                ve.tensor_reduce(RED[t % 2][:, 32 * b:32 * b + 32], PROD[b % 2][:, :].rearrange("p (o e) -> p o e", e=E0), AX.X, ALU.add).then_inc(red_done, 1)

            def finish_chunk(k):
                ve.wait_ge(d_done, k + 2)
                xs = X[:, bass.ds(k * CH, CH)].rearrange("p (r c) -> p r c", c=W)
                d = P1[:, bass.ds(k * (CR * PW), CR * PW)].rearrange("p (r c) -> p r c", c=PW)[:, :, 0:W]
                ve.tensor_tensor(xs, d, xs, ALU.add).then_inc(x1_done, 1)
                ve.wait_ge(x1_done, k + 1)
                ve.bn_stats(ST[:, bass.ds(k, 1), :], xs).then_inc(st_done, 1)

            def product(t, b, m, pt):
                ve.wait_ge(t_done, m + 1)
                if not isinstance(m, int) or m >= 2:
                    ve.wait_ge(red_done, m - 1)
                ve.tensor_tensor(PROD[b % 2][:, :].rearrange("p (o e) -> p o e", e=E0), ps[b][:, :].rearrange("p (o e) -> p o e", e=E0),
                                 PT[:, pt].rearrange("p (a e) -> p a e", a=1).broadcast_to([P, C, E0]), ALU.mult).then_inc(mult_done, 1)

            def block0(it, first):
                for half in range(2):
                    for t in range(4):
                        g = it * 8 + 4 * half + t
                        for b in range(B):
                            m = 4 * g + b
                            product(t, b, m, bass.ds(it * CH + t * P + half * 64 + b * E0, E0))
                            if b > 0:
                                if b == 1 and not (first and half == 0 and t < 2):
                                    ve.wait_ge(tr_done, g - 1)
                                reduce(half, t, b - 1, m - 1)
                            elif not (first and half == 0 and t == 0):
                                reduce(half, (t - 1) % 4, 3, m - 1)
                        if t == 1 and not first:
                            finish_chunk(2 * it + half - 2)

            block0(0, True)
            with ve.Fori(1, 4) as it:
                block0(it, False)
            for b in range(B):
                product(0, b, 128 + b, slice(4 * CH + b * E0, 4 * CH + (b + 1) * E0))
                if b == 1:
                    ve.wait_ge(tr_done, 31)
                reduce(0, 0 if b else 3, (b - 1) % 4, 127 + b)
            reduce(0, 0, 3, 131)
            finish_chunk(6)
            finish_chunk(7)
            ve.wait_ge(st_done, NCH)

            def normalise(k0):
                for k in range(0, NCH, 2):
                    ve.tensor_scalar(rows(IMG, 1 + k * CR, CR), X[:, k * CH:(k + 1) * CH].rearrange("p (r c) -> p r c", c=W),
                                     MV[:, 0:1], RS[:, 0:1], ALU.subtract, ALU.mult).then_inc(img_v, 1)

            coefs(2)
            ve.wait_ge(nmr_done, 2)
            ve.sem_inc(coef_ready, 1)
            normalise(0)
            for k in range(NCH):
                ve.wait_ge(c1_done, k + 1)
                xs = X[:, k * CH:(k + 1) * CH]
                ve.wait_ge(img_a, 4)
                ve.wait_ge(img_v, 4)
                ve.tensor_tensor(xs, ps[k % 4][:, :], xs, ALU.add).then_inc(x2_done, 1)
                ve.wait_ge(x2_done, k + 1)
                ins = ve.bn_stats(ST[:, k, :], xs)
            step(ins)
            coefs(3)
            ve.wait_ge(nmr_done, 3)
            ve.sem_inc(coef_ready, 1)
            ve.tensor_scalar(rows(CI, 1, 4), X[:, 0:4 * W].rearrange("p (r c) -> p r c", c=W), MV[:, 0:1], RS[:, 0:1], ALU.subtract, ALU.mult).then_inc(ci_done, 1)
            step(ve.memset(S1[:, 4, :], 0.0))
            step(ve.memset(S1[:, 4, 0:6:3], (NPIX - B * 5 * W) / 2.0))
            for b in range(B):
                ve.wait_ge(k1_done, b + 1)
                ins = ve.bn_stats(S1[:, b, :], ps[b][:, 0:5 * W])
            step(ins)
            step(ve.bn_aggr(M2[:, 0, :], S1[:, :, :]))
            ve.tensor_scalar(Q2[:, 7, 0:1], M2[:, 0, 1:2], EPS, None, ALU.add).then_inc(bm_ready, 1)
            step(ve.tensor_tensor(M2[:, 1, 0:1], M2[:, 0, 0:1], PAR[:, B1:B1 + 1], ALU.add))
            step(ve.tensor_tensor(M2[:, 1, 1:2], PAR[:, B1:B1 + 1], M2[:, 1, 0:1], ALU.subtract))
            ve.wait_ge(bm_done, 1)
            step(ve.tensor_tensor(Q2[:, 7, 2:3], Q2[:, 7, 1:2], PAR[:, G1:G1 + 1], ALU.mult))
            ve.scalar_tensor_tensor(Q2[:, 7, 3:4], M2[:, 1, 1:2], Q2[:, 7, 2:3], PAR[:, BE1:BE1 + 1], ALU.mult, ALU.add).then_inc(sh1_ready, 1)
            for e in range(NE):
                ve.wait_ge(k2_done, e + 1)
                ve.bn_stats(S2[:, e, 0, :], ps[e][:, 0:6 * W])
                ve.bn_stats(S2[:, e, 1, :], ps[e][:, 6 * W:7 * W])
                ins = ve.bn_stats(S2[:, e, 2, :], ps[e][:, 7 * W:8 * W])
            step(ins)
            for i in (0, 2, 3, 5):
                ins = ve.tensor_scalar(S2[:, :, 1, i:i + 1], S2[:, :, 1, i:i + 1], float(REP), None, ALU.mult)
            step(ins)
            for e in range(NE):
                ins = ve.bn_aggr(M2[:, e, :], S2[:, e, :, :])
            step(ins)
            ve.tensor_copy(Q2[:, 0, :], M2[:, :, 0]).then_inc(bm_ready, 1)
            ve.wait_ge(sh_avg, 1)
            step(ve.tensor_copy(Q2[:, 1, :], ps[4][:, 0:NE]))
            step(ve.tensor_tensor(Q2[:, 2, :], Q2[:, 0, :], Q2[:, 1, :], ALU.subtract))
            step(ve.tensor_tensor(Q2[:, 2, :], Q2[:, 2, :], Q2[:, 2, :], ALU.mult))
            ve.tensor_tensor(Q2[:, 2, :], Q2[:, 2, :], M2[:, :, 1], ALU.add).then_inc(bm_ready, 1)
            ve.wait_ge(sh_avg, 2)
            ve.tensor_scalar(Q2[:, 3, :], ps[4][:, 8:8 + NE], EPS, None, ALU.add).then_inc(bm_ready, 1)
            step(ve.tensor_tensor(Q2[:, 1, :], Q2[:, 1, :], PAR[:, B2:B2 + NE], ALU.add))
            step(ve.tensor_tensor(Q2[:, 1, :], PAR[:, B2:B2 + NE], Q2[:, 1, :], ALU.subtract))
            ve.wait_ge(bm_done, 2)
            step(ve.tensor_tensor(Q2[:, 5, :], Q2[:, 4, :], PAR[:, G2:G2 + NE], ALU.mult))
            step(ve.tensor_tensor(Q2[:, 6, :], Q2[:, 1, :], Q2[:, 5, :], ALU.mult))
            ve.tensor_tensor(Q2[:, 6, :], Q2[:, 6, :], PAR[:, BE2:BE2 + NE], ALU.add).then_inc(sh2_ready, 1)
            ve.wait_ge(z_done, NE)
            for j, c in enumerate((0, 1, W - 1)):
                ins = ve.tensor_scalar(NA[:, :, j], Z[:, :, 6 * W + c], -1.0, None, ALU.mult)
            step(ins)
            for j in range(3):
                ins = ve.tensor_reduce(AS[:, j:j + 1], NA[:, :, j], AX.X, ALU.add, negate=True)
            ins.then_inc(as_ready, 1)
            ve.wait_ge(u2_done, 1)
            for r0, r1, z0 in ((0, 6, 0), (H - 1, H, 7 * W)):
                a, m = r0 * W, (r1 - r0) * W
                for e in range(NE):
                    step(ve.tensor_tensor(T2[e][:, 0:m], U[:, a:a + m], Z[:, e, z0:z0 + m], ALU.add))
                    step(ve.scalar_tensor_tensor(X[:, a:a + m], T2[e][:, 0:m], 0.0, X[:, a:a + m], ALU.max, ALU.add))
            ve.wait_ge(xa_done, 3)
            uin = U[:, 6 * W:(H - 1) * W].rearrange("p (r c) -> p r c", c=W)
            xin = X[:, 6 * W:(H - 1) * W].rearrange("p (r c) -> p r c", c=W)
            for e in range(NE):
                for j, (c0, c1) in enumerate(((0, 1), (1, W - 1), (W - 1, W))):
                    ins = ve.scalar_tensor_tensor(xin[:, :, c0:c1], uin[:, :, c0:c1], NA[:, e, j:j + 1], xin[:, :, c0:c1], ALU.max, ALU.add)
                step(ins)
            for k in range(NCH):
                ins = ve.bn_stats(ST[:, k, :], X[:, k * CH:(k + 1) * CH])
            step(ins)
            coefs(4)
            ve.wait_ge(nmr_done, 4)
            ve.sem_inc(coef_ready, 1)
            normalise(1)
            for k in range(NCH):
                ve.wait_ge(c4_done, k + 1)
                if k >= 4:
                    ve.wait_ge(o_done, k - 3)
                ve.scalar_tensor_tensor(T2[k % 4][:, :].rearrange("p (r c) -> p r c", c=W), ps[k % 4][:, :].rearrange("p (r c) -> p r c", c=W),
                                        S3[:, 2:3], rows(IMG, 1 + k * CR, CR), ALU.mult, ALU.add).then_inc(t4_done, 1)


def kernel(**inputs):
    import numpy as np
    import concourse.bacc as bacc
    from concourse.bass_utils import run_bass_kernel_spmd as run

    g = {k: np.asarray(v) for k, v in inputs.items()}
    col = lambda a: np.tile(a, P // a.size).reshape(P, 1)
    row = lambda a: np.broadcast_to(a.reshape(1, -1), (P, a.size))
    eo = lambda a: np.tile(a.T, (B, 1))
    par = np.concatenate(
        [col(g['L0_conv_pb']), col(g['L0_conv_cb'])]
        + [g['L2_conv_' + n].reshape(P, 1) for n in ('b1', 'gamma1', 'beta1')]
        + [eo(g['L2_conv_' + n]) for n in ('b2', 'gamma2', 'beta2')]
        + [col(g['L3_conv_bn%d_%s' % (i, n)]) for i in (1, 2) for n in ('gamma', 'beta', 'mean', 'var')]
        + [row(g['L3_conv_alpha']), row(g['L1_conv_tap_offsets'][:, 0]), row(g['L1_conv_tap_offsets'][:, 1])], axis=1)
    arrays = {
        'x': g['x'].reshape(P, PIX),
        'w0': g['L0_conv_W'].reshape(C, C, TAPS, E0).transpose(2, 1, 0, 3).reshape(TAPS, C, C * E0),
        'pw': np.broadcast_to(g['L0_conv_pw'].reshape(E0, C).T[:, None, :], (C, 2, E0)),
        'cw': g['L0_conv_cw'].transpose(1, 2, 3, 0),
        'w1': g['L1_conv_weights'].transpose(1, 0, 2),
        'w2a': g['L2_conv_w1'].transpose(4, 2, 3, 0, 1).reshape(96, 3, NE * C),
        'w2b': g['L2_conv_w2'].transpose(4, 2, 0, 3, 1).reshape(96, NE, 3, C),
        'w3a': g['L3_conv_w1'].transpose(4, 2, 0, 3, 1).reshape(96, NM, 3 * C),
        'w3b': g['L3_conv_w2'].transpose(4, 2, 0, 3, 1).reshape(96, NM, 3 * C),
        'par': par,
    }
    nc = bacc.Bacc("TRN2", target_bir_lowering=False, num_devices=1)
    ins, args = {}, []
    for name, a in arrays.items():
        ins['in_' + name] = np.ascontiguousarray(a)
        args.append(nc.dram_tensor('in_' + name, a.shape, F32, kind="ExternalInput").ap())
    args.append(nc.dram_tensor("out_x", (P, PIX), F32, kind="ExternalOutput").ap())
    build(nc, *args)
    r = run(nc, [ins], core_ids=[0])
    return r.results[0]["out_x"].reshape(B, C, H, W)
```

```python
from contextlib import ExitStack

import concourse.bass as bass
from concourse import mybir

F32 = mybir.dt.float32
F32R = mybir.dt.float32r
ALU = mybir.AluOpType
ACT = mybir.ActivationFunctionType
AX = mybir.AxisListType

B, C, H, W = 4, 32, 64, 64
P = B * C
PIX = H * W
E0 = 16
NE = 4
NM = 10
TAPS = 9
PW = W + 2
PH = 68
CH = 512
NCH = PIX // CH
CR = CH // W
EPS = 1e-5
SPAN = 2 * PW + 2
S0 = CH + SPAN - 2
TAIL = H * PW - NCH * CH
CROWS = 8
PROWS = 14
REP = H - CROWS + 1
QI = CROWS + 2
NIMG = PH * PW
NPIX = B * PIX

SHARE4_V = [(b, g) for b in range(B) for g in range(4)][:10]
SHARE4_A = [(b, g) for b in range(B) for g in range(4)][10:]
SHARE3_V = [(b, g) for b in range(B) for g in range(3)][:8]
SHARE3_A = [(b, g) for b in range(B) for g in range(3)][8:]
HALVES = ((6, 27), (27, H - 1 - PROWS))


def span(g):
    return max(g - 1, 0), max(1 - g, 0), W - abs(g - 1)


PB, CB, B1, G1, BE1, B2, G2, BE2 = 0, 1, 2, 3, 4, 5, 9, 13
N1G, N1B, N1M, N1V, N2G, N2B, N2M, N2V, AL, DY, DX = 17, 18, 19, 20, 21, 22, 23, 24, 25, 35, 44
NPAR = 53


def build(nc, x, w0, pw, cw, w1, w2a, w2b, w3a, w3b, par, out):
    ctx = ExitStack()
    with ctx:
        cursor = [nc.sbuf_base]

        def sb(name, shape, dt=F32, at=None):
            size = 4
            for n in shape[1:]:
                size *= n
            size = -(-size // 32) * 32
            if at is None:
                at = -(-cursor[0] // 32) * 32
                cursor[0] = at + size
            return nc.alloc_sbuf_tensor_at(name, shape, dt, offset=at), at, at + size

        def sem(name):
            return ctx.enter_context(nc.semaphore(name))

        X = sb("X", [P, PIX])[0]
        U = sb("U", [P, PIX])[0]
        IMG = sb("IMG", [P, PH * PW])[0]
        PAR = sb("PAR", [P, NPAR])[0]
        ST = sb("ST", [P, NCH, 6])[0]
        MV = sb("MV", [P, 2])[0]
        VE = sb("VE", [P, 1])[0]
        RS = sb("RS", [P, 1])[0]
        NMR = sb("NMR", [P, 1])[0]
        MHALF = sb("MHALF", [P, 4])[0]
        WE = sb("WE", [P, 4, C])[0]
        W1R = sb("W1R", [P, C, TAPS])[0]
        CO = sb("CO", [P, 4, TAPS])[0]
        CX = sb("CX", [P, TAPS])[0]
        XG = sb("XG", [P, 1])[0]
        CT = sb("CT", [P, TAPS])[0]
        WT = sb("WT", [P, C, TAPS])[0]
        W2A = sb("W2A", [P, 3, NE * C])[0]
        W2B = sb("W2B", [P, NE, 3, C])[0]
        W3A = sb("W3A", [P, 3 * C])[0]
        W3B = sb("W3B", [P, 3 * C])[0]
        AVG = sb("AVG", [P, B, C])[0]
        ID = sb("ID", [P, P])[0]
        S3 = sb("S3", [P, 8])[0]
        top = cursor[0]
        HI, a, b_ = sb("HI", [P, PH * PW], F32R)
        LO = sb("LO", [P, PH * PW], F32R)[0]
        P1 = sb("P1", [P, PH * PW])[0]
        HS = [sb(f"HS{i}", [P, B, S0], F32R)[0] for i in range(2)]
        LS = [sb(f"LS{i}", [P, B, S0], F32R)[0] for i in range(2)]
        WA = sb("WA", [P, 3, CH], F32R)[0]
        WB = sb("WB", [96, 3, CH], F32R)[0]
        WC = sb("WC", [P, 2, CH], F32R)[0]
        RA, ra_at, _ = sb("RA", [P, 3, CH])
        RC = sb("RC", [P, 2, CH])[0]
        PWB = sb("PWB", [P, 2, B, E0])[0]
        CWB = sb("CWB", [P, 6, B, E0])[0]
        PARA = sb("PARA", [P, 5, CH])[0]
        PT = sb("PT", [P, 4 * CH + 64], at=ra_at)[0]
        PROD = [sb(f"PROD{i}", [P, CH])[0] for i in range(2)]
        RED = [sb(f"RED{i}", [P, P])[0] for i in range(2)]
        WR3 = sb("WR3", [96, NM, 3 * C])[0]
        WR3B = sb("WR3B", [96, NM, 3 * C])[0]
        assert cursor[0] <= nc.sbuf_usable_end, (cursor[0], nc.sbuf_usable_end)
        hi_end = cursor[0]
        cursor[0] = top
        SKF = sb("SK", [P, B * NIMG])[0]
        SK = SKF[:, :].rearrange("p (b n) -> p b n", b=B)
        SH = SKF[:, 0:NE * B * QI * W].rearrange("p (e b n) -> p e b n", e=NE, b=B)
        H1 = sb("H1", [P, B, CROWS * W])[0]
        CS = sb("CS", [P, B, 7 * W])[0]
        Z = sb("Z", [P, NE, CH])[0]
        T2 = [sb(f"T2{i}", [P, CH])[0] for i in range(4)]
        RR = [sb(f"RR{i}", [P, PROWS * (W - 2)])[0] for i in range(2)]
        IMG2 = sb("IMG2", [P, PH * PW])[0]
        S1 = sb("S1", [P, 5, 6])[0]
        S2 = sb("S2", [P, NE, 3, 6])[0]
        M2 = sb("M2", [P, NE, 2])[0]
        Q2 = sb("Q2", [P, 8, NE])[0]
        NA = sb("NA", [P, NE, 3])[0]
        AS = sb("AS", [P, 3])[0]
        OT = [sb(f"OT{i}", [P, CH])[0] for i in range(4)]
        assert cursor[0] <= hi_end

        ps = [ctx.enter_context(nc.psum_tensor(f"ps{i}", [P, CH], F32)) for i in range(8)]

        x_in = [sem(f"x_in{i}") for i in range(4)]
        w_pw, w_cw, w_main, w_par, w_l1, w_l2, w_l3 = (sem(f"w_{n}") for n in ("pw", "cw", "main", "par", "l1", "l2", "l3"))
        zeroed = sem("zeroed")
        wsplit = sem("wsplit")
        wl1_ready = sem("wl1_ready")
        wl3_ready = sem("wl3_ready")
        pstep = sem("pstep")
        vstep = sem("vstep")
        var_ready = sem("var_ready")
        rstd_ready = sem("rstd_ready")
        coef_ready = sem("coef_ready")
        u0_done = sem("u0_done")
        hi_done = sem("hi_done")
        lo_done = sem("lo_done")
        pw_done = sem("pw_done")
        p1_done = sem("p1_done")
        para_done = sem("para_done")
        para_sb = sem("para_sb")
        pt_done = sem("pt_done")
        pt_sb = sem("pt_sb")
        strip0 = [sem(f"strip0_{i}") for i in range(2)]
        t_done = sem("t_done")
        mult_done = sem("mult_done")
        red_done = sem("red_done")
        tr_done = sem("tr_done")
        x1_done = sem("x1_done")
        img_v = sem("img_v")
        img_a = sem("img_a")
        sk_pads = sem("sk_pads")
        e1_v = sem("e1_v")
        e1_a = sem("e1_a")
        part1 = [sem(f"part1_{i}") for i in range(2)]
        c1_done = sem("c1_done")
        x2_done = sem("x2_done")
        u2_done = sem("u2_done")
        k1_done = sem("k1_done")
        sh1_ready = sem("sh1_ready")
        k2_done = sem("k2_done")
        bm_ready = sem("bm_ready")
        bm_done = sem("bm_done")
        sh2_ready = sem("sh2_ready")
        z_done = sem("z_done")
        e3_v = sem("e3_v")
        e3_a = sem("e3_a")
        part3 = [sem(f"part3_{i}") for i in range(2)]
        c3_done = sem("c3_done")
        g_done = sem("g_done")
        part4 = [sem(f"part4_{i}") for i in range(3)]
        cs_v = sem("cs_v")
        cs_a = sem("cs_a")
        h1_v = sem("h1_v")
        h1_a = sem("h1_a")
        sh_v = sem("sh_v")
        sh_a = sem("sh_a")
        t2_done = sem("t2_done")
        rr_done = sem("rr_done")
        rp_done = sem("rp_done")
        xs_done = sem("xs_done")
        xh_done = sem("xh_done")
        na_ready = sem("na_ready")
        edge_done = sem("edge_done")
        c4_done = sem("c4_done")
        t4_done = sem("t4_done")
        r4_done = sem("r4_done")
        o_done = sem("o_done")
        x3_done = sem("x3_done")
        out_done = [sem(f"out_done{i}") for i in range(4)]
        st_done = sem("st_done")
        sh_avg = sem("sh_avg")
        d_done = sem("d_done")

        def rows(ap, r, n, c=1, w=W):
            return ap[:, r * PW:(r + n) * PW].rearrange("p (r c) -> p r c", c=PW)[:, :, c:c + w]

        def hidden_copy(e, g):
            pixel0, col0, width = span(g)
            src = H1[32 * e:32 * e + 32, :, :].rearrange("p b (r c) -> p b r c", c=W)[:, :, :, pixel0:pixel0 + width]
            dst = SH[32 * g:32 * g + 32, e, :, W:(1 + CROWS) * W].rearrange("p b (r c) -> p b r c", c=W)[:, :, :, col0:col0 + width]
            return dst, src

        block = ctx.enter_context(nc.Block())

        @block.sync
        def _(sp):
            for i in range(4):
                sp.dma_start(X[:, i * 1024:(i + 1) * 1024], x[:, i * 1024:(i + 1) * 1024]).then_inc(x_in[i], 16)
            sp.dma_start(PAR[:, :], par).then_inc(w_par, 16)
            for g in range(3):
                sp.dma_start(RA[32 * g:32 * g + 32, :, :], w0[g:9:3, :, :].rearrange("t c n -> c t n")).then_inc(w_main, 16)
            sp.dma_start(RA[96:128, :, :], w0[0:9:3, :, :].rearrange("t c n -> c t n")).then_inc(w_main, 16)
            for g, tap in enumerate((1, 2, 4, 5)):
                sp.dma_start(RC[32 * g:32 * g + 32, 0, :], w0[tap, :, :]).then_inc(w_main, 16)
            for g, tap in enumerate((7, 8)):
                sp.dma_start(RC[32 * g:32 * g + 32, 1, :], w0[tap, :, :]).then_inc(w_main, 16)
            sp.dma_start(W2A[0:96, :, :], w2a).then_inc(w_l2, 16)
            sp.dma_start(W2B[0:96, :, :, :], w2b).then_inc(w_l2, 16)
            sp.dma_start(WR3[:, :, :], w3a).then_inc(w_l3, 16)
            sp.dma_start(WR3B[:, :, :], w3b).then_inc(w_l3, 16)
            for g in range(4):
                sp.dma_start(W1R[32 * g:32 * g + 32, :, :], w1).then_inc(w_l1, 16)

            def strip_block0(s, half, n):
                for b in range(B):
                    pb = slice(32 * b, 32 * b + 32)
                    hs, ls = HS[half], LS[half]
                    copies = [(hs, g, HI, g, n + 2 * PW) for g in range(3)] + [(hs, 3, LO, 0, n + 2 * PW)]
                    copies += [(ls, g, LO, off, n + 2 * PW if g < 2 else n) for g, off in enumerate((1, 2, PW + 1, PW + 2))]
                    for dst, g, src, off, m in copies:
                        sp.dma_start(dst[32 * g:32 * g + 32, b, 0:m].bitcast(F32),
                                     src[pb, bass.ds(s * CH + off, m)].bitcast(F32)).then_inc(strip0[half], 16)

            for half in range(2):
                sp.wait_ge(lo_done, half + 2)
                strip_block0(half, half, CH)
            sp.wait_ge(lo_done, NCH)
            with sp.Fori(1, 4) as it:
                for half in range(2):
                    sp.wait_ge(t_done, 32 * it - 16 + 16 * half)
                    strip_block0(2 * it + half, half, CH)
            sp.wait_ge(t_done, 16 * 7)
            strip_block0(NCH, 0, TAIL)

            def copy_rows(img, groups, r0, r1, ready):
                n = (r1 - r0 - 1) * PW + W
                for b in range(B):
                    for g in range(groups):
                        a = r0 * PW
                        sp.dma_start(SK[32 * g:32 * g + 32, b, a:a + n], img[32 * b:32 * b + 32, a + g:a + g + n]).then_inc(ready, 16)

            sp.wait_ge(img_v, 2)
            sp.wait_ge(img_a, 2)
            copy_rows(IMG, 4, 19, 43, part1[0])
            sp.wait_ge(img_v, 3)
            sp.wait_ge(img_a, 3)
            copy_rows(IMG, 4, 43, 67, part1[1])
            sp.wait_ge(img_v, 5)
            sp.wait_ge(img_a, 5)
            copy_rows(IMG, 3, 18, 42, part3[0])
            sp.wait_ge(img_v, 6)
            sp.wait_ge(img_a, 6)
            copy_rows(IMG, 3, 42, 66, part3[1])
            for i, (r0, r1, k) in enumerate(((0, 18, 3), (18, 42, 6), (42, 66, 8))):
                sp.wait_ge(g_done, k)
                copy_rows(IMG2, 3, r0, r1, part4[i])
            for k in range(NCH):
                sp.wait_ge(o_done, k + 1)
                sp.dma_start(out[:, k * CH:(k + 1) * CH], OT[k % 4][:, :]).then_inc(out_done[k % 4], 16)
            for i in range(4):
                sp.wait_ge(out_done[i], 16 * NCH // 4)

        @block.gpsimd
        def _(gp):
            n = [0]

            def step(ins):
                n[0] += 1
                ins.then_inc(pstep, 1)
                gp.wait_ge(pstep, n[0])

            gp.memset(PWB[:, :, :, :], 0.0).then_inc(zeroed, 1)
            gp.memset(CWB[:, :, :, :], 0.0).then_inc(zeroed, 1)
            gp.memset(P1[:, :], 0.0).then_inc(zeroed, 1)
            for m in (HI, LO, IMG):
                gp.memset(m[:, 0:PW + 1].bitcast(F32), 0.0).then_inc(zeroed, 1)
                gp.memset(m[:, PW + W + 1:(H + 1) * PW + W + 1].bitcast(F32).rearrange("p (r c) -> p r c", c=PW)[:, :, 0:PW - W], 0.0).then_inc(zeroed, 1)
                gp.memset(m[:, (H + 1) * PW + 1:PH * PW].bitcast(F32), 0.0).then_inc(zeroed, 1)
            gp.memset(MHALF[:, :], -0.5).then_inc(zeroed, 1)
            step(gp.memset(ID[:, :], 0.0))
            step(gp.affine_select(out=ID[:, :], in_=ID[:, :], compare_op=ALU.not_equal, fill=1.0, base=0,
                                  pattern=[[-1, P]], channel_multiplier=1))
            for w in (W2A[96:128, :, :], W2B[96:128, :, :, :], W3A[96:128, :], W3B[96:128, :]):
                gp.memset(w, 0.0).then_inc(zeroed, 1)
            gp.wait_ge(zeroed, 17)

            def rstd(k):
                gp.wait_ge(var_ready, k)
                gp.tensor_tensor(RS[:, :], VE[:, :], MHALF[:, 0:1], ALU.pow).then_inc(rstd_ready, 1)
                gp.wait_ge(rstd_ready, k)

            rstd(1)
            for k in range(NCH):
                gp.wait_ge(hi_done, k + 1)
                gp.tensor_tensor(rows(LO, 1 + k * CR, CR), U[:, k * CH:(k + 1) * CH].rearrange("p (r c) -> p r c", c=W),
                                 rows(HI, 1 + k * CR, CR).bitcast(F32), ALU.subtract).then_inc(lo_done, 1)

            step(gp.memset(AVG[:, :, :], 0.0))
            for b in range(B):
                step(gp.affine_select(out=AVG[:, :, :], in_=AVG[:, :, :], compare_op=ALU.not_equal, fill=1.0 / B,
                                      base=-32 * b, pattern=[[0, B], [-1, C]], channel_multiplier=1))
            gp.wait_ge(w_par, 16)
            for g in range(4):
                step(gp.memset(XG[32 * g:32 * g + 32, :], float(g)))

            step(gp.tensor_scalar(CX[:, :], PAR[:, DX:DX + TAPS], XG[:, 0:1], None, ALU.subtract))
            step(gp.tensor_scalar(CT[:, :], CX[:, :], -1.0, 1.0, ALU.mult, ALU.add))
            step(gp.tensor_scalar(CX[:, :], CX[:, :], 1.0, 1.0, ALU.mult, ALU.add))
            step(gp.tensor_tensor(CT[:, :], CT[:, :], CX[:, :], ALU.subtract))
            step(gp.tensor_scalar(CT[:, :], CT[:, :], 0.0, None, ALU.min))
            step(gp.tensor_tensor(CX[:, :], CX[:, :], CT[:, :], ALU.add))
            step(gp.tensor_scalar(CX[:, :], CX[:, :], 0.0, None, ALU.max))
            for y in range(4):
                cy = CO[:, y, :]
                step(gp.tensor_scalar(CT[:, :], PAR[:, DY:DY + TAPS], -1.0, 1.0 + y, ALU.mult, ALU.add))
                step(gp.tensor_scalar(cy, PAR[:, DY:DY + TAPS], 1.0, 1.0 - y, ALU.mult, ALU.add))
                step(gp.tensor_tensor(CT[:, :], CT[:, :], cy, ALU.subtract))
                step(gp.tensor_scalar(CT[:, :], CT[:, :], 0.0, None, ALU.min))
                step(gp.tensor_tensor(cy, cy, CT[:, :], ALU.add))
                step(gp.tensor_scalar(cy, cy, 0.0, None, ALU.max))
                step(gp.tensor_tensor(cy, cy, CX[:, :], ALU.mult))
            gp.wait_ge(w_l1, 64)
            for y in range(4):
                step(gp.tensor_tensor(WT[:, :, :], W1R[:, :, :], CO[:, y:y + 1, :].broadcast_to([P, C, TAPS]), ALU.mult))
                for k in range(1, TAPS):
                    ins = gp.tensor_tensor(WT[:, :, 0] if k < TAPS - 1 else WE[:, y, :], WT[:, :, 0], WT[:, :, k], ALU.add)
                    step(ins)
            gp.memset(CT[:, :], 0.0).then_inc(wl1_ready, 1)
            gp.wait_ge(w_l3, 32)
            for raw, eff in ((WR3, W3A[0:96, :]), (WR3B, W3B[0:96, :])):
                step(gp.tensor_scalar(eff, raw[:, 0, :], PAR[0:96, AL:AL + 1], None, ALU.mult))
                for e in range(1, NM):
                    step(gp.tensor_scalar(raw[:, e, :], raw[:, e, :], PAR[0:96, AL + e:AL + e + 1], None, ALU.mult))
                    step(gp.tensor_tensor(eff, eff, raw[:, e, :], ALU.add))
            for i, (g, be, m, v) in enumerate(((N1G, N1B, N1M, N1V), (N2G, N2B, N2M, N2V))):
                sc, sh = S3[:, 2 * i:2 * i + 1], S3[:, 2 * i + 1:2 * i + 2]
                step(gp.tensor_scalar(sc, PAR[:, v:v + 1], 1.0, EPS, ALU.mult, ALU.add))
                step(gp.tensor_tensor(sc, sc, MHALF[:, 0:1], ALU.pow))
                step(gp.tensor_tensor(sc, sc, PAR[:, g:g + 1], ALU.mult))
                step(gp.tensor_tensor(sh, PAR[:, m:m + 1], sc, ALU.mult))
                step(gp.tensor_tensor(sh, PAR[:, be:be + 1], sh, ALU.subtract))
            gp.memset(CT[:, :], 0.0).then_inc(wl3_ready, 1)
            def clear_pads(last):
                gp.memset(SK[:, :, 0:PW], 0.0).then_inc(sk_pads, 1)
                sk = SK[:, :, PW:19 * PW].rearrange("p b (r c) -> p b r c", c=PW)
                gp.memset(sk[:, :, :, 0:1], 0.0).then_inc(sk_pads, 1)
                gp.memset(sk[:, :, :, W - last:W], 0.0).then_inc(sk_pads, 1)

            gp.wait_ge(t_done, 132)
            clear_pads(2)
            rstd(2)
            for m in (CS[:, :, :], IMG2[:, :]):
                gp.memset(m, 0.0).then_inc(zeroed, 1)
            gp.wait_ge(c1_done, NCH)
            for e in range(NE):
                gp.memset(SH[:, e, :, 0:W], 0.0).then_inc(zeroed, 1)
            rstd(3)
            sh = SH[:, :, :, :].rearrange("p e b (r c) -> p (e b) r c", c=W)
            gp.memset(SH[96:128, :, :, :], 0.0).then_inc(zeroed, 1)
            gp.wait_ge(zeroed, 24)
            gp.memset(sh[0:96, :, QI - 1, :], 0.0).then_inc(zeroed, 1)
            gp.wait_ge(zeroed, 25)
            gp.memset(sh[0:96, :, :, 0], 0.0).then_inc(zeroed, 1)
            gp.wait_ge(zeroed, 26)
            gp.memset(sh[0:96, :, :, W - 1], 0.0).then_inc(zeroed, 1)
            gp.wait_ge(zeroed, 27)
            gp.wait_ge(bm_ready, 1)
            gp.tensor_tensor(Q2[:, 7, 1:2], Q2[:, 7, 0:1], MHALF[:, 0:1], ALU.pow).then_inc(bm_done, 1)
            gp.wait_ge(bm_ready, 4)
            gp.tensor_tensor(Q2[:, 4, :], Q2[:, 3, :], MHALF[:, :], ALU.pow).then_inc(bm_done, 1)
            gp.wait_ge(k2_done, NE)
            clear_pads(1)
            gp.wait_ge(u2_done, 1)
            for e in range(NE):
                gp.wait_ge(z_done, e + 1)
                gp.tensor_tensor(T2[e][:, 0:6 * W], U[:, 0:6 * W], Z[:, e, 0:6 * W], ALU.add)
                gp.tensor_tensor(T2[e][:, 6 * W:7 * W], U[:, (H - 1) * W:PIX], Z[:, e, 7 * W:8 * W], ALU.add).then_inc(t2_done, 1)
            xp = X[:, (H - 1 - PROWS) * W:(H - 1) * W].rearrange("p (r c) -> p r c", c=W)[:, :, 1:W - 1]
            for e in range(NE):
                gp.wait_ge(rr_done, e + 1)
                if e:
                    gp.wait_ge(rp_done, e)
                gp.tensor_tensor(xp, xp, RR[e % 2][:, :].rearrange("p (r c) -> p r c", c=W - 2), ALU.add).then_inc(rp_done, 1)
            rstd(4)
            for k in range(NCH):
                gp.wait_ge(r4_done, k + 1)
                if k >= 4:
                    gp.wait_ge(out_done[k % 4], 16 * (k // 4))
                gp.tensor_tensor(OT[k % 4][:, :], T2[k % 4][:, :], X[:, k * CH:(k + 1) * CH], ALU.add).then_inc(o_done, 1)

        @block.scalar
        def _(act):
            act.wait_ge(zeroed, 2)
            for b in range(B):
                act.dma_start(PWB[32 * b:32 * b + 32, :, b, :], pw).then_inc(w_pw, 16)
            for b in range(B):
                act.dma_start(CWB[16 * b:16 * b + 16, 0:3, b, :], cw[:, 0, :, :]).then_inc(w_cw, 16)
                act.dma_start(CWB[64 + 16 * b:80 + 16 * b, 0:3, b, :], cw[:, 1, :, :]).then_inc(w_cw, 16)
                act.dma_start(CWB[16 * b:16 * b + 16, 3:6, b, :], cw[:, 2, :, :]).then_inc(w_cw, 16)
            act.wait_ge(zeroed, 13)
            for k in range(NCH):
                act.wait_ge(u0_done, k + 1)
                act.activation(rows(HI, 1 + k * CR, CR), U[:, k * CH:(k + 1) * CH].rearrange("p (r c) -> p r c", c=W), ACT.Copy).then_inc(hi_done, 1)
            for k in range(NCH):
                act.wait_ge(pw_done, k + 1)
                if k == 0:
                    act.wait_ge(w_par, 16)
                src = ps[6 + k % 2]
                for d in range(2):
                    p = slice(64 * d, 64 * d + 64)
                    act.activation(rows(P1[p, :], 1 - d + k * CR, CR), src[p, :].rearrange("p (r c) -> p r c", c=W), ACT.Relu,
                                   bias=PAR[p, PB:PB + 1]).then_inc(p1_done, 1)
            for q in range(4):
                act.wait_ge(para_done, q + 1)
                act.activation(PARA[:, q, :], ps[4 + q % 2][:, :], ACT.Identity, bias=PAR[:, CB:CB + 1]).then_inc(para_sb, 1)
            act.wait_ge(para_done, 5)
            act.activation(PARA[0:64, 4, 0:TAIL], ps[4][0:64, 0:TAIL], ACT.Identity, bias=PAR[0:64, CB:CB + 1]).then_inc(para_sb, 1)
            with act.Fori(0, 4) as it:
                for half in range(2):
                    act.wait_ge(tr_done, 8 * it + 4 * half + 4)
                    act.activation(P1[:, bass.ds(it * 2 * CH + half * CH, CH)], ps[4 + half][:, :], ACT.Copy).then_inc(d_done, 1)
            act.wait_ge(tr_done, 33)
            act.activation(P1[:, NCH * CH:NCH * CH + TAIL], ps[4][:, 0:TAIL], ACT.Copy).then_inc(d_done, 1)

            def norm(out_ap, k0, k1, p=slice(0, P), c0=0, c1=W):
                return act.activation(out_ap, X[p, k0 * W:k1 * W].rearrange("p (r c) -> p r c", c=W)[:, :, c0:c1], ACT.Identity,
                                      bias=NMR[p, 0:1], scale=RS[p, 0:1])

            def image_and_stack(base, groups, first_rows, share, own):
                act.wait_ge(coef_ready, base)
                for k in (3, 5):
                    norm(rows(IMG, 1 + k * CR, CR), k * CR, (k + 1) * CR).then_inc(img_a, 1)
                act.wait_ge(sk_pads, 3 if groups == 4 else 6)
                for n, (r0, r1) in enumerate(((0, first_rows), (first_rows, first_rows + CR))):
                    for b, g in share:
                        pixel0, col0, width = span(g)
                        ins = norm(SK[32 * g:32 * g + 32, b, (1 + r0) * PW:(1 + r1) * PW].rearrange("p (r c) -> p r c", c=PW)[:, :, col0:col0 + width],
                                   r0, r1, slice(32 * b, 32 * b + 32), pixel0, pixel0 + width)
                    ins.then_inc(own, 1)
                    if n == 0:
                        norm(rows(IMG, 1 + 7 * CR, CR), 7 * CR, 8 * CR).then_inc(img_a, 1)

            image_and_stack(1, 4, CR + 2, SHARE4_A, e1_a)
            act.wait_ge(coef_ready, 2)
            act.wait_ge(zeroed, 19)
            for b, g in SHARE3_A:
                pixel0, col0, width = span(g)
                ins = norm(CS[32 * g:32 * g + 32, b, W:5 * W].rearrange("p (r c) -> p r c", c=W)[:, :, col0:col0 + width],
                           0, 4, slice(32 * b, 32 * b + 32), pixel0, pixel0 + width)
            ins.then_inc(cs_a, 1)
            act.activation(U[:, :], X[:, :], ACT.Identity, bias=NMR[:, 0:1], scale=RS[:, 0:1]).then_inc(u2_done, 1)
            act.wait_ge(sh1_ready, 1)
            for b in (1, 3):
                act.activation(H1[:, b, 0:5 * W], ps[b][:, 0:5 * W], ACT.Relu, bias=Q2[:, 7, 3:4], scale=Q2[:, 7, 2:3]).then_inc(h1_a, 1)
            act.wait_ge(h1_v, 3)
            act.wait_ge(h1_a, 2)
            act.wait_ge(zeroed, 27)
            for e in range(NE):
                act.activation(*hidden_copy(e, 0), ACT.Copy).then_inc(sh_a, 1)
            act.wait_ge(sh2_ready, 1)
            for e in range(NE):
                act.activation(Z[:, e, :], ps[e][:, :], ACT.Identity, bias=Q2[:, 6, e:e + 1], scale=Q2[:, 5, e:e + 1]).then_inc(z_done, 1)
            act.wait_ge(na_ready, 1)
            up = U[:, (H - 1 - PROWS) * W:(H - 1) * W].rearrange("p (r c) -> p r c", c=W)[:, :, 1:W - 1]
            for e in range(NE):
                if e >= 2:
                    act.wait_ge(rp_done, e - 1)
                act.activation(RR[e % 2][:, :].rearrange("p (r c) -> p r c", c=W - 2), up, ACT.Relu, bias=Z[:, e, 6 * W + 1:6 * W + 2]).then_inc(rr_done, 1)
                if e == 1:
                    act.wait_ge(edge_done, 1)
                    xe = X[:, 6 * W:(H - 1) * W].rearrange("p (r c) -> p r c", c=W)
                    act.activation(xe[:, :, 0:1], xe[:, :, 0:1], ACT.Identity, bias=AS[:, 0:1]).then_inc(xs_done, 1)
                    act.activation(xe[:, :, W - 1:W], xe[:, :, W - 1:W], ACT.Identity, bias=AS[:, 2:3]).then_inc(xs_done, 1)
            for i, (r0, r1) in enumerate(HALVES):
                act.wait_ge(xh_done, i + 1)
                xh = X[:, r0 * W:r1 * W].rearrange("p (r c) -> p r c", c=W)[:, :, 1:W - 1]
                act.activation(xh, xh, ACT.Identity, bias=AS[:, 1:2]).then_inc(xs_done, 1)
            image_and_stack(3, 3, CR + 1, SHARE3_A, e3_a)
            act.wait_ge(wl3_ready, 1)
            act.wait_ge(zeroed, 19)
            for k in range(NCH):
                act.wait_ge(c3_done, k + 1)
                act.activation(rows(IMG2, 1 + k * CR, CR), ps[k % 4][:, :].rearrange("p (r c) -> p r c", c=W), ACT.Relu,
                               bias=S3[:, 1:2], scale=S3[:, 0:1]).then_inc(g_done, 1)
            for k in range(NCH):
                act.wait_ge(t4_done, k + 1)
                act.activation(T2[k % 4][:, :], T2[k % 4][:, :], ACT.Relu, bias=S3[:, 3:4]).then_inc(r4_done, 1)

        @block.tensor
        def _(pe):
            pe.wait_ge(w_pw, 64)
            for k in range(NCH):
                pe.wait_ge(u0_done, k + 1)
                if k >= 2:
                    pe.wait_ge(p1_done, 2 * (k - 1))
                pe.matmul(ps[6 + k % 2][:, :], PWB[:, :, :, :], U[:, k * CH:(k + 1) * CH], start=True, stop=True).then_inc(pw_done, 1)
            pe.wait_ge(w_cw, 192)
            for q in range(5):
                pe.wait_ge(p1_done, min(4 * q + 6, 16))
                if q >= 2:
                    pe.wait_ge(para_sb, q - 1)
                n = CH if q < 4 else TAIL
                for i in range(6):
                    for h in range(2 if q < 4 else 1):
                        a = (2 * q + h) * CH + i % 3 + (0 if i < 3 else 2 * PW)
                        ins = pe.matmul(ps[4 + q % 2][64 * h:64 * h + 64, 0:n], CWB[:, i, :, :], P1[:, a:a + n],
                                        start=(i == 0), stop=(i == 5))
                ins.then_inc(para_done, 1)
            for q in range(5):
                pe.wait_ge(para_sb, q + 1)
                if q >= 2:
                    pe.wait_ge(pt_sb, q - 1)
                k = P if q < 4 else 64
                for t in range(4 if q < 4 else 1):
                    ins = pe.transpose(ps[6 + q % 2][:, t * P:t * P + k], PARA[0:k, q, t * P:(t + 1) * P], ID[0:k, 0:k])
                ins.then_inc(pt_done, 1)

            def tile(half, t, b):
                px = lambda s, off, k=P: s[half][0:k, b, off + t * P:off + (t + 1) * P]
                for dy in range(3):
                    pe.matmul(ps[b][:, :], px(HS, dy * PW), WA[:, dy, :], start=(dy == 0), stop=False)
                    pe.matmul(ps[b][:, :], px(HS, dy * PW, 96), WB[:, dy, :], start=False, stop=False)
                pe.matmul(ps[b][:, :], px(LS, 0), WC[:, 0, :], start=False, stop=False)
                pe.matmul(ps[b][:, :], px(LS, 2 * PW, 64), WC[0:64, 1, :], start=False, stop=True).then_inc(t_done, 1)

            def back(half, t, g, strip, first=False):
                pe.wait_ge(red_done, 4 * g + 4)
                if t == 0 and not first:
                    pe.wait_ge(d_done, strip - 1)
                pe.transpose(ps[4 + half][:, t * P:(t + 1) * P], RED[t % 2][:, :], ID[:, :]).then_inc(tr_done, 1)

            def block0(it, first):
                for half in range(2):
                    pe.wait_ge(strip0[half], 16 * 32 * (it + 1))
                    for t in range(4):
                        g = it * 8 + 4 * half + t
                        for b in range(B):
                            if not (first and 4 * half + t == 0):
                                pe.wait_ge(mult_done, 4 * g + b - 3)
                            tile(half, t, b)
                        if t > 0:
                            back(half, t - 1, g - 1, 2 * it + half, first)
                        elif not (first and half == 0):
                            back(1 - half, 3, g - 1, 0)

            pe.wait_ge(wsplit, 3)
            block0(0, True)
            with pe.Fori(1, 4) as it:
                block0(it, False)
            pe.wait_ge(strip0[0], 16 * 32 * 5)
            for b in range(B):
                pe.wait_ge(mult_done, 4 * 32 + b - 3)
                tile(0, 0, b)
            back(1, 3, 31, 7)
            back(0, 0, 32, 8)

            def conv(k, wt, slots, done):
                for y in range(slots):
                    for b in range(B):
                        ins = pe.matmul(ps[k % 4][32 * b:32 * b + 32, :], wt(y), rows(SK[:, b, :], k * CR + y, CR, 0),
                                        start=(y == 0), stop=(y == slots - 1))
                ins.then_inc(done, 1)

            def engine_rows(k, ev, ea):
                if k < 2:
                    pe.wait_ge(ev, k + 1)
                    pe.wait_ge(ea, k + 1)

            pe.wait_ge(wl1_ready, 1)
            for k in range(NCH):
                engine_rows(k, e1_v, e1_a)
                if k in (2, 5):
                    pe.wait_ge(part1[k // 5], 16 * 16)
                if k >= 4:
                    pe.wait_ge(x2_done, k - 3)
                conv(k, lambda y: WE[:, y, :], 4, c1_done)
            pe.wait_ge(w_l2, 32)
            pe.wait_ge(cs_v, 1)
            pe.wait_ge(cs_a, 1)
            for b in range(B):
                for dy in range(3):
                    ins = pe.matmul(ps[b][:, 0:5 * W], W2A[:, dy, :], CS[:, b, dy * W:(dy + 5) * W], start=(dy == 0), stop=(dy == 2))
                ins.then_inc(k1_done, 1)
            for e in range(NE):
                pe.wait_ge(sh_v, 2 * e + 2)
                pe.wait_ge(sh_a, e + 1)
                for dy in range(3):
                    for b in range(B):
                        ins = pe.matmul(ps[e][32 * b:32 * b + 32, :], W2B[:, e, dy, :], SH[:, e, b, dy * W:(dy + CROWS) * W],
                                        start=(dy == 0), stop=(dy == 2))
                ins.then_inc(k2_done, 1)
            for i, q in ((0, 0), (1, 2)):
                pe.wait_ge(bm_ready, 2 + i)
                pe.matmul(ps[4][:, 8 * i:8 * i + NE], AVG[:, :, :], Q2[:, q, :], start=True, stop=True).then_inc(sh_avg, 1)
            pe.wait_ge(wl3_ready, 1)
            for k in range(NCH):
                engine_rows(k, e3_v, e3_a)
                if k in (2, 5):
                    pe.wait_ge(part3[k // 5], 16 * 12)
                if k >= 4:
                    pe.wait_ge(g_done, k - 3)
                conv(k, lambda y: W3A[:, 32 * y:32 * y + 32], 3, c3_done)
            for k in range(NCH):
                if k in (0, 2, 5):
                    pe.wait_ge(part4[(k + 1) // 3], 16 * 12)
                pe.wait_ge(g_done, min(5 + k, NCH))
                if k >= 4:
                    pe.wait_ge(t4_done, k - 3)
                conv(k, lambda y: W3B[:, 32 * y:32 * y + 32], 3, c4_done)

        @block.vector
        def _(ve):
            n = [0]

            def step(ins):
                n[0] += 1
                ins.then_inc(vstep, 1)
                ve.wait_ge(vstep, n[0])

            def coefs(k):
                step(ve.bn_aggr(MV[:, :], ST[:, :, :]))
                ve.tensor_scalar(VE[:, :], MV[:, 1:2], EPS, None, ALU.add).then_inc(var_ready, 1)
                ve.wait_ge(rstd_ready, k)
                ins = ve.scalar_tensor_tensor(NMR[:, :], MV[:, 0:1], -1.0, RS[:, :], ALU.mult, ALU.mult)
                if k > 1:
                    ins.then_inc(coef_ready, 1)

            for k in range(NCH):
                if k % 2 == 0:
                    ve.wait_ge(x_in[k // 2], 16)
                ins = ve.bn_stats(ST[:, k, :], X[:, k * CH:(k + 1) * CH])
            step(ins)
            coefs(1)
            for k in range(NCH):
                ve.tensor_scalar(U[:, k * CH:(k + 1) * CH], X[:, k * CH:(k + 1) * CH], MV[:, 0:1], RS[:, 0:1], ALU.subtract, ALU.mult).then_inc(u0_done, 1)
            ve.wait_ge(w_main, 160)
            ve.tensor_copy(WA[:, :, :], RA[:, :, :]).then_inc(wsplit, 1)
            ve.tensor_copy(WC[:, 0, :], RC[:, 0, :])
            ve.tensor_copy(WC[0:64, 1, :], RC[0:64, 1, :]).then_inc(wsplit, 1)
            ve.wait_ge(wsplit, 2)
            ve.tensor_tensor(WB[:, :, :], RA[0:96, :, :], WA[0:96, :, :].bitcast(F32), ALU.subtract).then_inc(wsplit, 1)
            ve.wait_ge(wsplit, 3)
            for q in range(5):
                ve.wait_ge(pt_done, q + 1)
                n_pt = CH if q < 4 else 64
                ve.tensor_copy(PT[:, q * CH:q * CH + n_pt], ps[6 + q % 2][:, 0:n_pt]).then_inc(pt_sb, 1)
            ve.wait_ge(pt_sb, 5)

            def reduce(half, t, b, m):
                ve.wait_ge(mult_done, m + 1)
                ve.tensor_reduce(RED[t % 2][:, 32 * b:32 * b + 32], PROD[b % 2][:, :].rearrange("p (o e) -> p o e", e=E0), AX.X, ALU.add).then_inc(red_done, 1)

            def finish_chunk(k):
                ve.wait_ge(d_done, k + 2)
                xs = X[:, bass.ds(k * CH, CH)].rearrange("p (r c) -> p r c", c=W)
                d = P1[:, bass.ds(k * (CR * PW), CR * PW)].rearrange("p (r c) -> p r c", c=PW)[:, :, 0:W]
                ve.tensor_tensor(xs, d, xs, ALU.add).then_inc(x1_done, 1)
                ve.wait_ge(x1_done, k + 1)
                ve.bn_stats(ST[:, bass.ds(k, 1), :], xs).then_inc(st_done, 1)

            def product(t, b, m, pt):
                ve.wait_ge(t_done, m + 1)
                if not isinstance(m, int) or m >= 2:
                    ve.wait_ge(red_done, m - 1)
                ve.tensor_tensor(PROD[b % 2][:, :].rearrange("p (o e) -> p o e", e=E0), ps[b][:, :].rearrange("p (o e) -> p o e", e=E0),
                                 PT[:, pt].rearrange("p (a e) -> p a e", a=1).broadcast_to([P, C, E0]), ALU.mult).then_inc(mult_done, 1)

            def block0(it, first):
                for half in range(2):
                    for t in range(4):
                        g = it * 8 + 4 * half + t
                        for b in range(B):
                            m = 4 * g + b
                            product(t, b, m, bass.ds(it * CH + t * P + half * 64 + b * E0, E0))
                            if b > 0:
                                if b == 1 and not (first and half == 0 and t < 2):
                                    ve.wait_ge(tr_done, g - 1)
                                reduce(half, t, b - 1, m - 1)
                            elif not (first and half == 0 and t == 0):
                                reduce(half, (t - 1) % 4, 3, m - 1)
                        if t == 1 and not first:
                            finish_chunk(2 * it + half - 2)

            block0(0, True)
            with ve.Fori(1, 4) as it:
                block0(it, False)
            for b in range(B):
                product(0, b, 128 + b, slice(4 * CH + b * E0, 4 * CH + (b + 1) * E0))
                if b == 1:
                    ve.wait_ge(tr_done, 31)
                reduce(0, 0 if b else 3, (b - 1) % 4, 127 + b)
            reduce(0, 0, 3, 131)
            finish_chunk(6)
            finish_chunk(7)
            ve.wait_ge(st_done, NCH)

            def norm(out_ap, k0, k1, p=slice(0, P), c0=0, c1=W):
                return ve.tensor_scalar(out_ap, X[p, k0 * W:k1 * W].rearrange("p (r c) -> p r c", c=W)[:, :, c0:c1],
                                        MV[p, 0:1], RS[p, 0:1], ALU.subtract, ALU.mult)

            def image_and_stack(groups, first_rows, share, own, whole):
                for k in (2, 4):
                    norm(rows(IMG, 1 + k * CR, CR), k * CR, (k + 1) * CR).then_inc(img_v, 1)
                ve.wait_ge(sk_pads, 3 if groups == 4 else 6)
                for n, (r0, r1) in enumerate(((0, first_rows), (first_rows, first_rows + CR))):
                    for b, g in share:
                        pixel0, col0, width = span(g)
                        ins = norm(SK[32 * g:32 * g + 32, b, (1 + r0) * PW:(1 + r1) * PW].rearrange("p (r c) -> p r c", c=PW)[:, :, col0:col0 + width],
                                   r0, r1, slice(32 * b, 32 * b + 32), pixel0, pixel0 + width)
                    ins.then_inc(own, 1)
                    if n == 0:
                        norm(rows(IMG, 1 + 6 * CR, CR), 6 * CR, 7 * CR).then_inc(img_v, 1)
                if whole:
                    norm(rows(IMG, 1, 2 * CR), 0, 2 * CR).then_inc(img_v, 1)

            coefs(2)
            image_and_stack(4, CR + 2, SHARE4_V, e1_v, False)
            for k in range(NCH):
                ve.wait_ge(c1_done, k + 1)
                xs = X[:, k * CH:(k + 1) * CH]
                if k == 0:
                    ve.wait_ge(e1_v, 2)
                    ve.wait_ge(e1_a, 2)
                ve.tensor_tensor(xs, ps[k % 4][:, :], xs, ALU.add).then_inc(x2_done, 1)
                ve.wait_ge(x2_done, k + 1)
                ins = ve.bn_stats(ST[:, k, :], xs)
            step(ins)
            coefs(3)
            ve.wait_ge(zeroed, 19)
            for b, g in SHARE3_V:
                pixel0, col0, width = span(g)
                ins = norm(CS[32 * g:32 * g + 32, b, W:5 * W].rearrange("p (r c) -> p r c", c=W)[:, :, col0:col0 + width],
                           0, 4, slice(32 * b, 32 * b + 32), pixel0, pixel0 + width)
            ins.then_inc(cs_v, 1)
            step(ve.memset(S1[:, 4, :], 0.0))
            step(ve.memset(S1[:, 4, 0:6:3], (NPIX - B * 5 * W) / 2.0))
            for b in range(B):
                ve.wait_ge(k1_done, b + 1)
                ins = ve.bn_stats(S1[:, b, :], ps[b][:, 0:5 * W])
            step(ins)
            step(ve.bn_aggr(M2[:, 0, :], S1[:, :, :]))
            ve.tensor_scalar(Q2[:, 7, 0:1], M2[:, 0, 1:2], EPS, None, ALU.add).then_inc(bm_ready, 1)
            step(ve.tensor_tensor(M2[:, 1, 0:1], M2[:, 0, 0:1], PAR[:, B1:B1 + 1], ALU.add))
            step(ve.tensor_tensor(M2[:, 1, 1:2], PAR[:, B1:B1 + 1], M2[:, 1, 0:1], ALU.subtract))
            ve.wait_ge(bm_done, 1)
            step(ve.tensor_tensor(Q2[:, 7, 2:3], Q2[:, 7, 1:2], PAR[:, G1:G1 + 1], ALU.mult))
            ve.scalar_tensor_tensor(Q2[:, 7, 3:4], M2[:, 1, 1:2], Q2[:, 7, 2:3], PAR[:, BE1:BE1 + 1], ALU.mult, ALU.add).then_inc(sh1_ready, 1)
            ve.wait_ge(sh1_ready, 1)
            for b in (0, 2):
                step(ve.tensor_scalar(H1[:, b, 0:5 * W], ps[b][:, 0:5 * W], Q2[:, 7, 2:3], Q2[:, 7, 3:4], ALU.mult, ALU.add))
                ve.tensor_scalar(H1[:, b, 0:5 * W], H1[:, b, 0:5 * W], 0.0, None, ALU.max).then_inc(h1_v, 1)
            ve.tensor_scalar(H1[:, :, 5 * W:CROWS * W], Q2[:, 7, 3:4].rearrange("p (a c) -> p a c", a=1).broadcast_to([P, B, 3 * W]), 0.0, None, ALU.max).then_inc(h1_v, 1)
            ve.wait_ge(h1_v, 3)
            ve.wait_ge(h1_a, 2)
            ve.wait_ge(zeroed, 27)
            for e in range(NE):
                for g in (1, 2):
                    ve.tensor_copy(*hidden_copy(e, g)).then_inc(sh_v, 1)
            for e in range(NE):
                ve.wait_ge(k2_done, e + 1)
                ve.bn_stats(S2[:, e, 0, :], ps[e][:, 0:6 * W])
                ve.bn_stats(S2[:, e, 1, :], ps[e][:, 6 * W:7 * W])
                ins = ve.bn_stats(S2[:, e, 2, :], ps[e][:, 7 * W:8 * W])
            step(ins)
            for i in (0, 2, 3, 5):
                ins = ve.tensor_scalar(S2[:, :, 1, i:i + 1], S2[:, :, 1, i:i + 1], float(REP), None, ALU.mult)
            step(ins)
            for e in range(NE):
                ins = ve.bn_aggr(M2[:, e, :], S2[:, e, :, :])
            step(ins)
            ve.tensor_copy(Q2[:, 0, :], M2[:, :, 0]).then_inc(bm_ready, 1)
            ve.wait_ge(sh_avg, 1)
            step(ve.tensor_copy(Q2[:, 1, :], ps[4][:, 0:NE]))
            step(ve.tensor_tensor(Q2[:, 2, :], Q2[:, 0, :], Q2[:, 1, :], ALU.subtract))
            step(ve.tensor_tensor(Q2[:, 2, :], Q2[:, 2, :], Q2[:, 2, :], ALU.mult))
            ve.tensor_tensor(Q2[:, 2, :], Q2[:, 2, :], M2[:, :, 1], ALU.add).then_inc(bm_ready, 1)
            ve.wait_ge(sh_avg, 2)
            ve.tensor_scalar(Q2[:, 3, :], ps[4][:, 8:8 + NE], EPS, None, ALU.add).then_inc(bm_ready, 1)
            step(ve.tensor_tensor(Q2[:, 1, :], Q2[:, 1, :], PAR[:, B2:B2 + NE], ALU.add))
            step(ve.tensor_tensor(Q2[:, 1, :], PAR[:, B2:B2 + NE], Q2[:, 1, :], ALU.subtract))
            ve.wait_ge(bm_done, 2)
            step(ve.tensor_tensor(Q2[:, 5, :], Q2[:, 4, :], PAR[:, G2:G2 + NE], ALU.mult))
            step(ve.tensor_tensor(Q2[:, 6, :], Q2[:, 1, :], Q2[:, 5, :], ALU.mult))
            ve.tensor_tensor(Q2[:, 6, :], Q2[:, 6, :], PAR[:, BE2:BE2 + NE], ALU.add).then_inc(sh2_ready, 1)
            ve.wait_ge(z_done, NE)
            for j, c in enumerate((0, 1, W - 1)):
                ins = ve.tensor_scalar(NA[:, :, j], Z[:, :, 6 * W + c], -1.0, None, ALU.mult)
            step(ins)
            for j in range(3):
                ins = ve.tensor_reduce(AS[:, j:j + 1], NA[:, :, j], AX.X, ALU.add, negate=True)
            ins.then_inc(na_ready, 1)
            ve.wait_ge(u2_done, 1)
            for j, c in ((0, 0), (2, W - 1)):
                uc, xc = (m[:, 6 * W:(H - 1) * W].rearrange("p (r c) -> p r c", c=W)[:, :, c:c + 1] for m in (U, X))
                for e in range(NE):
                    ins = ve.scalar_tensor_tensor(xc, uc, NA[:, e, j:j + 1], xc, ALU.max, ALU.add)
                    if (j, e) == (2, NE - 1):
                        ins.then_inc(edge_done, 1)
                    else:
                        step(ins)
            for i, (r0, r1) in enumerate(HALVES):
                uh, xh = (m[:, r0 * W:r1 * W].rearrange("p (r c) -> p r c", c=W)[:, :, 1:W - 1] for m in (U, X))
                for e in range(NE):
                    ins = ve.scalar_tensor_tensor(xh, uh, NA[:, e, 1:2], xh, ALU.max, ALU.add)
                    if e < NE - 1:
                        step(ins)
                ins.then_inc(xh_done, 1)
                if i == 0:
                    for a, m, t0 in ((0, 6 * W, 0), ((H - 1) * W, W, 6 * W)):
                        for e in range(NE):
                            ve.wait_ge(t2_done, e + 1)
                            step(ve.scalar_tensor_tensor(X[:, a:a + m], T2[e][:, t0:t0 + m], 0.0, X[:, a:a + m], ALU.max, ALU.add))
                    ve.wait_ge(xs_done, 3)
                    for k in range(0, 3):
                        ve.bn_stats(ST[:, k, :], X[:, k * CH:(k + 1) * CH])
            ve.wait_ge(rp_done, NE)
            step(ve.bn_stats(ST[:, 7, :], X[:, 7 * CH:8 * CH]))
            ve.wait_ge(xs_done, 4)
            for k in range(3, 7):
                ins = ve.bn_stats(ST[:, k, :], X[:, k * CH:(k + 1) * CH])
            step(ins)
            coefs(4)
            image_and_stack(3, CR + 1, SHARE3_V, e3_v, True)
            ve.wait_ge(img_v, 7)
            ve.wait_ge(img_a, 6)
            for k in range(NCH):
                ve.wait_ge(c4_done, k + 1)
                if k >= 4:
                    ve.wait_ge(o_done, k - 3)
                ve.scalar_tensor_tensor(T2[k % 4][:, :].rearrange("p (r c) -> p r c", c=W), ps[k % 4][:, :].rearrange("p (r c) -> p r c", c=W),
                                        S3[:, 2:3], rows(IMG, 1 + k * CR, CR), ALU.mult, ALU.add).then_inc(t4_done, 1)


def kernel(**inputs):
    import numpy as np
    import concourse.bacc as bacc
    from concourse.bass_utils import run_bass_kernel_spmd as run

    g = {k: np.asarray(v) for k, v in inputs.items()}
    col = lambda a: np.tile(a, P // a.size).reshape(P, 1)
    row = lambda a: np.broadcast_to(a.reshape(1, -1), (P, a.size))
    eo = lambda a: np.tile(a.T, (B, 1))
    par = np.concatenate(
        [col(g['L0_conv_pb']), col(g['L0_conv_cb'])]
        + [g['L2_conv_' + n].reshape(P, 1) for n in ('b1', 'gamma1', 'beta1')]
        + [eo(g['L2_conv_' + n]) for n in ('b2', 'gamma2', 'beta2')]
        + [col(g['L3_conv_bn%d_%s' % (i, n)]) for i in (1, 2) for n in ('gamma', 'beta', 'mean', 'var')]
        + [row(g['L3_conv_alpha']), row(g['L1_conv_tap_offsets'][:, 0]), row(g['L1_conv_tap_offsets'][:, 1])], axis=1)
    arrays = {
        'x': g['x'].reshape(P, PIX),
        'w0': g['L0_conv_W'].reshape(C, C, TAPS, E0).transpose(2, 1, 0, 3).reshape(TAPS, C, C * E0),
        'pw': np.broadcast_to(g['L0_conv_pw'].reshape(E0, C).T[:, None, :], (C, 2, E0)),
        'cw': g['L0_conv_cw'].transpose(1, 2, 3, 0),
        'w1': g['L1_conv_weights'].transpose(1, 0, 2),
        'w2a': g['L2_conv_w1'].transpose(4, 2, 3, 0, 1).reshape(96, 3, NE * C),
        'w2b': g['L2_conv_w2'].transpose(4, 2, 0, 3, 1).reshape(96, NE, 3, C),
        'w3a': g['L3_conv_w1'].transpose(4, 2, 0, 3, 1).reshape(96, NM, 3 * C),
        'w3b': g['L3_conv_w2'].transpose(4, 2, 0, 3, 1).reshape(96, NM, 3 * C),
        'par': par,
    }
    nc = bacc.Bacc("TRN2", target_bir_lowering=False, num_devices=1)
    ins, args = {}, []
    for name, a in arrays.items():
        ins['in_' + name] = np.ascontiguousarray(a)
        args.append(nc.dram_tensor('in_' + name, a.shape, F32, kind="ExternalInput").ap())
    args.append(nc.dram_tensor("out_x", (P, PIX), F32, kind="ExternalOutput").ap())
    build(nc, *args)
    r = run(nc, [ins], core_ids=[0])
    return r.results[0]["out_x"].reshape(B, C, H, W)
```

```python
from contextlib import ExitStack

import concourse.bass as bass
from concourse import mybir

F32 = mybir.dt.float32
F32R = mybir.dt.float32r
I32 = mybir.dt.int32
ALU = mybir.AluOpType
ACT = mybir.ActivationFunctionType
AX = mybir.AxisListType

B, C, H, W = 4, 32, 64, 64
P = B * C
PIX = H * W
E0 = 16
NE = 4
NM = 10
TAPS = 9
PW = W + 2
PH = 68
CH = 512
NCH = PIX // CH
CR = CH // W
EPS = 1e-5
NT = H * PW // P
STRIP_T = 5
SL = STRIP_T * P
S0 = SL + 2 * PW
TIT = 2 * STRIP_T
STEPS = NT // TIT
REST = NT - STEPS * TIT
NDMA = 21
CROWS = 8
PROWS = 22
REP = H - CROWS + 1
QI = CROWS + 2
NIMG = PH * PW
NPIX = B * PIX
WIN = 3
FAR = H + 1
FROWS = 2 * FAR + H + 1
FCOLS = 2 * FAR + PW + 1

Z_DIAG = 2
Z_BORDER = Z_DIAG + 1 + 2 * 3 + 1
Z_WEIGHT = Z_BORDER + 4
Z_IMAGE = Z_WEIGHT + 3
Z_LATER = Z_IMAGE + 2
Z_HIDDEN = Z_LATER + NE + 4

SHARE4_V = [(b, g) for b in range(B) for g in range(4)][:10]
SHARE4_A = [(b, g) for b in range(B) for g in range(4)][10:]
SHARE3_V = [(b, g) for b in range(B) for g in range(3)][:8]
SHARE3_A = [(b, g) for b in range(B) for g in range(3)][8:]
PARTS = ((6, 24), (24, H - 1 - PROWS))


def span(g):
    return max(g - 1, 0), max(1 - g, 0), W - abs(g - 1)


PB, CB, B1, G1, BE1, B2, G2, BE2 = 0, 1, 2, 3, 4, 5, 9, 13
N1G, N1B, N1M, N1V, N2G, N2B, N2M, N2V, AL, DY, DX = 17, 18, 19, 20, 21, 22, 23, 24, 25, 35, 44
NPAR = 53


def build(nc, x, w0, pw, cw, w1, w2a, w2b, w3a, w3b, par, out):
    ctx = ExitStack()
    with ctx:
        cursor = [nc.sbuf_base]

        def sb(name, shape, dt=F32, at=None):
            size = 4
            for n in shape[1:]:
                size *= n
            size = -(-size // 32) * 32
            if at is None:
                at = -(-cursor[0] // 32) * 32
                cursor[0] = at + size
            return nc.alloc_sbuf_tensor_at(name, shape, dt, offset=at), at, at + size

        def sem(name):
            return ctx.enter_context(nc.semaphore(name))

        X = sb("X", [P, PIX])[0]
        U, u_at, _ = sb("U", [P, PIX])
        IMG, img_at, _ = sb("IMG", [P, PH * PW])
        PAR = sb("PAR", [P, NPAR])[0]
        ST = sb("ST", [P, NCH, 6])[0]
        MV = sb("MV", [P, 2])[0]
        VE = sb("VE", [P, 1])[0]
        RS = sb("RS", [P, 1])[0]
        NMR = sb("NMR", [P, 1])[0]
        MHALF = sb("MHALF", [P, 4])[0]
        WE = sb("WE", [P, 4, C])[0]
        W1R = sb("W1R", [P, C, TAPS])[0]
        CO = sb("CO", [P, 4, TAPS])[0]
        CX = sb("CX", [P, TAPS])[0]
        XG = sb("XG", [P, 1])[0]
        CT = sb("CT", [P, TAPS])[0]
        OFF = sb("OFF", [P, 4, 2 * TAPS])[0]
        OFI = sb("OFI", [P, 2 * TAPS], I32)[0]
        FARN = sb("FARN", [P, 1], I32)[0]
        FC = sb("FC", [P, 4, TAPS])[0]
        INS = sb("INS", [P, 2])[0]
        WT = sb("WT", [P, C, TAPS])[0]
        W2A = sb("W2A", [P, 3, NE * C])[0]
        W2B = sb("W2B", [P, NE, 3, C])[0]
        W3A = sb("W3A", [P, 3 * C])[0]
        W3B = sb("W3B", [P, 3 * C])[0]
        AVG = sb("AVG", [P, B, C])[0]
        ID = sb("ID", [P, P])[0]
        S3 = sb("S3", [P, 8])[0]
        top = cursor[0]
        HI = sb("HI", [P, PH * PW], F32R)[0]
        LO = sb("LO", [P, PH * PW], F32R)[0]
        P1 = sb("P1", [P, PH * PW])[0]
        HS = [sb(f"HS{i}", [P, B, S0], F32R)[0] for i in range(2)]
        LS = [sb(f"LS{i}", [P, B, S0], F32R)[0] for i in range(2)]
        TS = [sb("TS0", [96, B, SL], F32R, at=img_at)[0], sb("TS1", [96, B, SL], F32R, at=u_at)[0]]
        WA = sb("WA", [P, 3, CH], F32R)[0]
        WB = sb("WB", [P, 3, CH], F32R)[0]
        WC = sb("WC", [96, CH], F32R)[0]
        PT, pt_at, _ = sb("PT", [P, 4 * CH + 64])
        RA = sb("RA", [P, 3, CH], at=pt_at)[0]
        PWB = sb("PWB", [P, 2, B, E0])[0]
        CWB = sb("CWB", [P, 6, 2, B, E0])[0]
        PARA, _, para_end = sb("PARA", [B * E0, H * PW])
        PROD = [sb(f"PROD{i}", [P, CH])[0] for i in range(2)]
        RED = [sb(f"RED{i}", [P, P])[0] for i in range(2)]
        WR3 = sb("WR3", [96, NM, 3 * C], at=para_end - NM * 3 * C * 4)[0]
        WR3B = sb("WR3B", [96, NM, 3 * C], at=para_end - 2 * NM * 3 * C * 4)[0]
        assert cursor[0] <= nc.sbuf_usable_end, (cursor[0], nc.sbuf_usable_end)
        hi_end = cursor[0]
        cursor[0] = top
        SKF, _, skf_end = sb("SK", [P, B * NIMG])
        SK = SKF[:, :].rearrange("p (b n) -> p b n", b=B)
        SH = SKF[:, 0:NE * B * QI * W].rearrange("p (e b n) -> p e b n", e=NE, b=B)
        H1 = sb("H1", [P, B, CROWS * W])[0]
        CS = sb("CS", [P, B, 7 * W])[0]
        Z = sb("Z", [P, NE, CH])[0]
        Z6 = sb("Z6", [P, NE, W])[0]
        T2 = [sb(f"T2{i}", [P, CH])[0] for i in range(4)]
        RR = [sb(f"RR{i}", [P, PROWS * (W - 2)])[0] for i in range(2)]
        IMG2 = sb("IMG2", [P, PH * PW])[0]
        S1 = sb("S1", [P, 5, 6])[0]
        S2 = sb("S2", [P, NE, 3, 6])[0]
        M2 = sb("M2", [P, NE, 2])[0]
        Q2 = sb("Q2", [P, 8, NE])[0]
        NA = sb("NA", [P, NE, 3])[0]
        AS = sb("AS", [P, 3])[0]
        OT = [sb(f"OT{i}", [P, CH])[0] for i in range(4)]
        assert cursor[0] <= hi_end
        cursor[0] = skf_end
        FE = sb("FE", [P, FROWS * PW])[0]
        FS = sb("FS", [P, CR + 1, FCOLS])[0]
        FW = sb("FW", [P, CR + 1, W + 1])[0]
        FB = sb("FB", [P, 4, P])[0]
        assert cursor[0] <= hi_end, (cursor[0], hi_end)

        ps = [ctx.enter_context(nc.psum_tensor(f"ps{i}", [P, CH], F32)) for i in range(8)]

        x_in = [sem(f"x_in{i}") for i in range(4)]
        w_pw, w_cw, w_main, w_par, w_l1, w_l2, w_l3 = (sem(f"w_{n}") for n in ("pw", "cw", "main", "par", "l1", "l2", "l3"))
        zeroed = sem("zeroed")
        w0_split = sem("w0_split")
        w1_mixed = sem("w1_mixed")
        w3_mixed = sem("w3_mixed")
        pool_step = sem("pool_step")
        vector_step = sem("vector_step")
        var_ready = sem("var_ready")
        rstd_ready = sem("rstd_ready")
        coef_ready = sem("coef_ready")
        norm0_done = sem("norm0_done")
        hi_done = sem("hi_done")
        lo_done = sem("lo_done")
        pw_conv_done = sem("pw_conv_done")
        p1_lower_done = sem("p1_lower_done")
        p1_upper_done = sem("p1_upper_done")
        para_conv_done = sem("para_conv_done")
        para_even_done = sem("para_even_done")
        para_odd_done = sem("para_odd_done")
        para_pads = sem("para_pads")
        pt_done = sem("pt_done")
        pt_in_sbuf = sem("pt_in_sbuf")
        strip_hi = [sem(f"strip_hi{i}") for i in range(2)]
        strip_ready = [sem(f"strip_ready{i}") for i in range(2)]
        tile_done = sem("tile_done")
        product_done = sem("product_done")
        sum_done = sem("sum_done")
        sums_transposed = sem("sums_transposed")
        x1_done = sem("x1_done")
        image_by_vector = sem("image_by_vector")
        image_by_scalar = sem("image_by_scalar")
        stack_pads_zeroed = sem("stack_pads_zeroed")
        stack1_by_vector = sem("stack1_by_vector")
        stack1_by_scalar = sem("stack1_by_scalar")
        stack1_by_dma = [sem(f"stack1_by_dma{i}") for i in range(2)]
        conv1_done = sem("conv1_done")
        x2_done = sem("x2_done")
        norm2_done = sem("norm2_done")
        masked_conv1_done = sem("masked_conv1_done")
        bn1_ready = sem("bn1_ready")
        masked_conv2_done = sem("masked_conv2_done")
        bn_input_ready = sem("bn_input_ready")
        bn_power_done = sem("bn_power_done")
        bn2_ready = sem("bn2_ready")
        z_done = sem("z_done")
        stack3_by_vector = sem("stack3_by_vector")
        stack3_by_scalar = sem("stack3_by_scalar")
        stack3_by_dma = [sem(f"stack3_by_dma{i}") for i in range(2)]
        conv3_done = sem("conv3_done")
        hidden3_done = sem("hidden3_done")
        stack4_by_dma = [sem(f"stack4_by_dma{i}") for i in range(3)]
        compact_by_vector = sem("compact_by_vector")
        compact_by_scalar = sem("compact_by_scalar")
        hidden_by_vector = sem("hidden_by_vector")
        hidden_by_scalar = sem("hidden_by_scalar")
        hidden_stack_by_vector = sem("hidden_stack_by_vector")
        hidden_stack_by_scalar = sem("hidden_stack_by_scalar")
        first_rows_added = sem("first_rows_added")
        pool_relu_done = sem("pool_relu_done")
        pool_rows_added = sem("pool_rows_added")
        z_sum_added = sem("z_sum_added")
        max_sum_done = sem("max_sum_done")
        minus_z_ready = sem("minus_z_ready")
        z_row6_done = sem("z_row6_done")
        conv4_done = sem("conv4_done")
        affine4_done = sem("affine4_done")
        out_rows_done = sem("out_rows_done")
        x3_shifted = sem("x3_shifted")
        out_written = [sem(f"out_written{i}") for i in range(4)]
        stats1_done = sem("stats1_done")
        averaged = sem("averaged")
        block0_in_sbuf = sem("block0_in_sbuf")
        far_known = sem("far_known")
        far_image = sem("far_image")
        far_weights = sem("far_weights")
        far_strip = sem("far_strip")
        far_window = sem("far_window")
        far_conv = sem("far_conv")
        far_added = sem("far_added")
        far_over = sem("far_over")

        def rows(ap, r, n, c=1, w=W):
            return ap[:, r * PW:(r + n) * PW].rearrange("p (r c) -> p r c", c=PW)[:, :, c:c + w]

        def para_rows(q, h):
            return PARA[:, 16 * q * PW:16 * (q + 1) * PW].rearrange("p (r h c) -> p r h c", h=2, c=PW)[:, :, h, 0:W]

        def pw_bank(k):
            return ps[(6, 7, 0, 1)[k % 4]]

        def pair_bank(pair):
            return ps[4 + pair % 4][:, 0:2 * P]

        def hidden_copy(e, g):
            pixel0, col0, width = span(g)
            src = H1[32 * e:32 * e + 32, :, :].rearrange("p b (r c) -> p b r c", c=W)[:, :, :, pixel0:pixel0 + width]
            dst = SH[32 * g:32 * g + 32, e, :, W:(1 + CROWS) * W].rearrange("p b (r c) -> p b r c", c=W)[:, :, :, col0:col0 + width]
            return dst, src

        block = ctx.enter_context(nc.Block())

        @block.sync
        def _(sp):
            for i in range(4):
                sp.dma_start(X[:, i * 1024:(i + 1) * 1024], x[:, i * 1024:(i + 1) * 1024]).then_inc(x_in[i], 16)
            sp.dma_start(PAR[:, :], par).then_inc(w_par, 16)
            sp.wait_ge(zeroed, Z_DIAG)
            for b in range(B):
                sp.dma_start(PWB[32 * b:32 * b + 32, :, b, :], pw).then_inc(w_pw, 16)
            for b in range(B):
                lo, up = slice(16 * b, 16 * b + 16), slice(64 + 16 * b, 80 + 16 * b)
                for p, slot, h, dy in ((lo, 0, 0, 0), (up, 0, 0, 1), (up, 0, 1, 0), (lo, 3, 0, 2), (lo, 3, 1, 1), (up, 3, 1, 2)):
                    sp.dma_start(CWB[p, slot:slot + 3, h, b, :], cw[:, dy, :, :]).then_inc(w_cw, 16)
            for g in range(3):
                sp.dma_start(RA[32 * g:32 * g + 32, :, :], w0[g:9:3, :, :].rearrange("t c n -> c t n")).then_inc(w_main, 16)
            sp.dma_start(RA[96:128, :, :], w0[0:9:3, :, :].rearrange("t c n -> c t n")).then_inc(w_main, 16)
            def stack_hi(s, half, n):
                m = n + 2 * PW
                for b in range(B):
                    for g in range(3):
                        sp.dma_start(HS[half][32 * g:32 * g + 32, b, 0:m].bitcast(F32),
                                     HI[32 * b:32 * b + 32, bass.ds(s * SL + g, m)].bitcast(F32)).then_inc(strip_hi[half], 16)

            def stack_lo(s, half, n):
                m = n + 2 * PW
                for b in range(B):
                    for g, stack in enumerate((HS, LS)):
                        sp.dma_start(stack[half][96:128, b, 0:m].bitcast(F32),
                                     LO[32 * b:32 * b + 32, bass.ds(s * SL + g, m)].bitcast(F32)).then_inc(strip_ready[half], 16)

            def stack_third(s, half, n):
                for b in range(B):
                    for dy in range(3):
                        sp.dma_start(TS[half][32 * dy:32 * dy + 32, b, 0:n].bitcast(F32),
                                     LO[32 * b:32 * b + 32, bass.ds(s * SL + dy * PW + 2, n)].bitcast(F32)).then_inc(strip_ready[half], 16)

            def repeat_hi(half, n, count):
                m = n + 2 * PW
                sp.wait_ge(strip_hi[half], 16 * 12 * count)
                sp.dma_start(LS[half][0:96, :, 0:m].bitcast(F32), HS[half][0:96, :, 0:m].bitcast(F32)).then_inc(strip_ready[half], 16)

            for half in range(2):
                sp.wait_ge(hi_done, half + 2)
                stack_hi(half, half, SL)
                sp.wait_ge(lo_done, half + 2)
                stack_lo(half, half, SL)
                if half:
                    sp.wait_ge(lo_done, NCH)
                    sp.wait_ge(pw_conv_done, NCH)
                stack_third(half, half, SL)
                repeat_hi(half, SL, 1)
            sp.dma_start(W2A[0:96, :, :], w2a).then_inc(w_l2, 16)
            sp.dma_start(W2B[0:96, :, :, :], w2b).then_inc(w_l2, 16)
            sp.wait_ge(pt_done, 5)
            sp.dma_start(WR3[:, :, :], w3a).then_inc(w_l3, 16)
            sp.dma_start(WR3B[:, :, :], w3b).then_inc(w_l3, 16)
            for g in range(4):
                sp.dma_start(W1R[32 * g:32 * g + 32, :, :], w1).then_inc(w_l1, 16)
            with sp.Fori(1, STEPS) as it:
                for half in range(2):
                    s = 2 * it + half
                    sp.wait_ge(tile_done, (2 * it + half - 1) * B * STRIP_T)
                    stack_hi(s, half, SL)
                    stack_lo(s, half, SL)
                    stack_third(s, half, SL)
                    repeat_hi(half, SL, it + 1)
            sp.wait_ge(tile_done, (2 * STEPS - 1) * B * STRIP_T)
            stack_hi(2 * STEPS, 0, REST * P)
            stack_lo(2 * STEPS, 0, REST * P)
            stack_third(2 * STEPS, 0, REST * P)
            repeat_hi(0, REST * P, STEPS + 1)

            def copy_rows(img, groups, r0, r1, ready):
                n = (r1 - r0 - 1) * PW + W
                for b in range(B):
                    for g in range(groups):
                        a = r0 * PW
                        sp.dma_start(SK[32 * g:32 * g + 32, b, a:a + n], img[32 * b:32 * b + 32, a + g:a + g + n]).then_inc(ready, 16)

            sp.wait_ge(zeroed, Z_IMAGE)
            sp.wait_ge(image_by_vector, 2)
            sp.wait_ge(image_by_scalar, 2)
            copy_rows(IMG, 4, 19, 43, stack1_by_dma[0])
            sp.wait_ge(image_by_vector, 3)
            sp.wait_ge(image_by_scalar, 3)
            copy_rows(IMG, 4, 43, 67, stack1_by_dma[1])
            sp.wait_ge(image_by_vector, 5)
            sp.wait_ge(image_by_scalar, 5)
            copy_rows(IMG, 3, 18, 42, stack3_by_dma[0])
            sp.wait_ge(image_by_vector, 6)
            sp.wait_ge(image_by_scalar, 6)
            copy_rows(IMG, 3, 42, 66, stack3_by_dma[1])
            for i, (r0, r1, k) in enumerate(((0, 18, 3), (18, 42, 6), (42, 66, 8))):
                sp.wait_ge(hidden3_done, k)
                copy_rows(IMG2, 3, r0, r1, stack4_by_dma[i])
            for k in range(NCH):
                sp.wait_ge(out_rows_done, k + 1)
                sp.dma_start(out[:, k * CH:(k + 1) * CH], OT[k % 4][:, :]).then_inc(out_written[k % 4], 16)
            for i in range(4):
                sp.wait_ge(out_written[i], 16 * NCH // 4)

        @block.gpsimd
        def _(gp):
            n = [0]

            def step(ins):
                n[0] += 1
                ins.then_inc(pool_step, 1)
                gp.wait_ge(pool_step, n[0])

            gp.memset(PWB[:, :, :, :], 0.0).then_inc(zeroed, 1)
            gp.memset(CWB[:, :, :, :], 0.0).then_inc(zeroed, 1)
            gp.memset(P1[:, :], 0.0).then_inc(zeroed, 1)
            gp.memset(PARA[:, :].rearrange("p (r c) -> p r c", c=PW)[:, :, W:PW], 0.0).then_inc(para_pads, 1)
            def clear_border(m):
                gp.memset(m[:, 0:PW + 1].bitcast(F32), 0.0).then_inc(zeroed, 1)
                gp.memset(m[:, PW + W + 1:(H + 1) * PW + W + 1].bitcast(F32).rearrange("p (r c) -> p r c", c=PW)[:, :, 0:PW - W], 0.0).then_inc(zeroed, 1)
                gp.memset(m[:, (H + 1) * PW + 1:PH * PW].bitcast(F32), 0.0).then_inc(zeroed, 1)

            clear_border(HI)
            clear_border(LO)
            gp.memset(MHALF[:, :], -0.5).then_inc(zeroed, 1)
            step(gp.memset(ID[:, :], 0.0))
            step(gp.affine_select(out=ID[:, :], in_=ID[:, :], compare_op=ALU.not_equal, fill=1.0, base=0,
                                  pattern=[[-1, P]], channel_multiplier=1))
            for w in (W2A[96:128, :, :], W2B[96:128, :, :, :], W3A[96:128, :], W3B[96:128, :]):
                gp.memset(w, 0.0).then_inc(zeroed, 1)
            gp.wait_ge(zeroed, Z_WEIGHT)

            def rstd(k):
                gp.wait_ge(var_ready, k)
                gp.tensor_tensor(RS[:, :], VE[:, :], MHALF[:, 0:1], ALU.pow).then_inc(rstd_ready, 1)
                gp.wait_ge(rstd_ready, k)

            rstd(1)
            for k in range(NCH):
                gp.wait_ge(hi_done, k + 1)
                gp.tensor_tensor(rows(LO, 1 + k * CR, CR), U[:, k * CH:(k + 1) * CH].rearrange("p (r c) -> p r c", c=W),
                                 rows(HI, 1 + k * CR, CR).bitcast(F32), ALU.subtract).then_inc(lo_done, 1)

            step(gp.memset(AVG[:, :, :], 0.0))
            for b in range(B):
                step(gp.affine_select(out=AVG[:, :, :], in_=AVG[:, :, :], compare_op=ALU.not_equal, fill=1.0 / B,
                                      base=-32 * b, pattern=[[0, B], [-1, C]], channel_multiplier=1))
            gp.wait_ge(w_par, 16)
            for g in range(4):
                step(gp.memset(XG[32 * g:32 * g + 32, :], float(g)))

            off = PAR[:, DY:DY + 2 * TAPS]
            lim, flo, fra, within = (OFF[:, i, :] for i in range(4))
            step(gp.tensor_scalar(lim, off, float(-FAR), float(FAR), ALU.max, ALU.min))
            step(gp.tensor_copy(OFI[:, :], lim))
            step(gp.tensor_copy(flo, OFI[:, :]))
            step(gp.tensor_tensor(fra, flo, lim, ALU.subtract))
            step(gp.tensor_scalar(fra, fra, 0.0, None, ALU.is_gt))
            step(gp.tensor_tensor(flo, flo, fra, ALU.subtract))
            step(gp.tensor_tensor(fra, lim, flo, ALU.subtract))
            step(gp.tensor_scalar(flo, flo, float(FAR), None, ALU.add))
            step(gp.tensor_copy(OFI[:, :], flo))
            step(gp.tensor_scalar(within, off, 0.0, None, ALU.is_ge))
            step(gp.tensor_scalar(lim, off, float(WIN), None, ALU.is_le))
            step(gp.tensor_tensor(within, within, lim, ALU.mult))
            step(gp.tensor_tensor(within[:, 0:TAPS], within[:, 0:TAPS], within[:, TAPS:2 * TAPS], ALU.mult))
            inside = within[:, 0:TAPS]
            step(gp.tensor_copy(INS[:, 0:1], inside[:, 0:1]))
            for k in range(1, TAPS):
                step(gp.tensor_tensor(INS[:, 0:1], INS[:, 0:1], inside[:, k:k + 1], ALU.mult))
            step(gp.tensor_scalar(INS[:, 1:2], INS[:, 0:1], -1.0, 1.0, ALU.mult, ALU.add))
            step(gp.tensor_scalar(within[:, TAPS:2 * TAPS], inside, -1.0, 1.0, ALU.mult, ALU.add))
            step(gp.tensor_scalar(lim, fra, -1.0, 1.0, ALU.mult, ALU.add))
            for s in range(4):
                fy, fx = (fra if s // 2 else lim)[:, 0:TAPS], (fra if s % 2 else lim)[:, TAPS:2 * TAPS]
                step(gp.tensor_tensor(FC[:, s, :], fy, fx, ALU.mult))
                step(gp.tensor_tensor(FC[:, s, :], FC[:, s, :], within[:, TAPS:2 * TAPS], ALU.mult))
            gp.tensor_copy(FARN[:, :], INS[:, 1:2]).then_inc(far_known, 1)
            step(gp.tensor_scalar(CX[:, :], PAR[:, DX:DX + TAPS], XG[:, 0:1], None, ALU.subtract))
            step(gp.tensor_scalar(CT[:, :], CX[:, :], -1.0, 1.0, ALU.mult, ALU.add))
            step(gp.tensor_scalar(CX[:, :], CX[:, :], 1.0, 1.0, ALU.mult, ALU.add))
            step(gp.tensor_tensor(CT[:, :], CT[:, :], CX[:, :], ALU.subtract))
            step(gp.tensor_scalar(CT[:, :], CT[:, :], 0.0, None, ALU.min))
            step(gp.tensor_tensor(CX[:, :], CX[:, :], CT[:, :], ALU.add))
            step(gp.tensor_scalar(CX[:, :], CX[:, :], 0.0, None, ALU.max))
            step(gp.tensor_tensor(CX[:, :], CX[:, :], inside, ALU.mult))
            for y in range(4):
                cy = CO[:, y, :]
                step(gp.tensor_scalar(CT[:, :], PAR[:, DY:DY + TAPS], -1.0, 1.0 + y, ALU.mult, ALU.add))
                step(gp.tensor_scalar(cy, PAR[:, DY:DY + TAPS], 1.0, 1.0 - y, ALU.mult, ALU.add))
                step(gp.tensor_tensor(CT[:, :], CT[:, :], cy, ALU.subtract))
                step(gp.tensor_scalar(CT[:, :], CT[:, :], 0.0, None, ALU.min))
                step(gp.tensor_tensor(cy, cy, CT[:, :], ALU.add))
                step(gp.tensor_scalar(cy, cy, 0.0, None, ALU.max))
                step(gp.tensor_tensor(cy, cy, CX[:, :], ALU.mult))
            gp.wait_ge(w_l1, 64)
            for y in range(4):
                step(gp.tensor_tensor(WT[:, :, :], W1R[:, :, :], CO[:, y:y + 1, :].broadcast_to([P, C, TAPS]), ALU.mult))
                for k in range(1, TAPS):
                    ins = gp.tensor_tensor(WT[:, :, 0] if k < TAPS - 1 else WE[:, y, :], WT[:, :, 0], WT[:, :, k], ALU.add)
                    step(ins)
            gp.memset(CT[:, :], 0.0).then_inc(w1_mixed, 1)
            gp.wait_ge(w_l3, 32)
            for raw, eff in ((WR3, W3A[0:96, :]), (WR3B, W3B[0:96, :])):
                step(gp.tensor_scalar(eff, raw[:, 0, :], PAR[0:96, AL:AL + 1], None, ALU.mult))
                for e in range(1, NM):
                    step(gp.tensor_scalar(raw[:, e, :], raw[:, e, :], PAR[0:96, AL + e:AL + e + 1], None, ALU.mult))
                    step(gp.tensor_tensor(eff, eff, raw[:, e, :], ALU.add))
            for i, (g, be, m, v) in enumerate(((N1G, N1B, N1M, N1V), (N2G, N2B, N2M, N2V))):
                sc, sh = S3[:, 2 * i:2 * i + 1], S3[:, 2 * i + 1:2 * i + 2]
                step(gp.tensor_scalar(sc, PAR[:, v:v + 1], 1.0, EPS, ALU.mult, ALU.add))
                step(gp.tensor_tensor(sc, sc, MHALF[:, 0:1], ALU.pow))
                step(gp.tensor_tensor(sc, sc, PAR[:, g:g + 1], ALU.mult))
                step(gp.tensor_tensor(sh, PAR[:, m:m + 1], sc, ALU.mult))
                step(gp.tensor_tensor(sh, PAR[:, be:be + 1], sh, ALU.subtract))
            step(gp.tensor_scalar(S3[:, 4:5], S3[:, 3:4], -1.0, None, ALU.mult))
            gp.memset(CT[:, :], 0.0).then_inc(w3_mixed, 1)
            def clear_pads(last):
                gp.memset(SK[:, :, 0:PW], 0.0).then_inc(stack_pads_zeroed, 1)
                sk = SK[:, :, PW:19 * PW].rearrange("p b (r c) -> p b r c", c=PW)
                gp.memset(sk[:, :, :, 0:1], 0.0).then_inc(stack_pads_zeroed, 1)
                gp.memset(sk[:, :, :, W - last:W], 0.0).then_inc(stack_pads_zeroed, 1)

            gp.wait_ge(tile_done, 132)
            clear_pads(2)
            clear_border(IMG)
            gp.wait_ge(zeroed, Z_IMAGE)
            rstd(2)
            gp.wait_ge(far_known, 1)
            far = gp.value_load(FARN[0:1, 0:1], min_val=0, max_val=1)
            with gp.If(far > 0):
                gp.wait_ge(far_over, 1)
            for m in (CS[:, :, :], IMG2[:, :]):
                gp.memset(m, 0.0).then_inc(zeroed, 1)
            gp.wait_ge(conv1_done, NCH)
            for e in range(NE):
                gp.memset(SH[:, e, :, 0:W], 0.0).then_inc(zeroed, 1)
            rstd(3)
            sh = SH[:, :, :, :].rearrange("p e b (r c) -> p (e b) r c", c=W)
            gp.memset(SH[96:128, :, :, :], 0.0).then_inc(zeroed, 1)
            gp.wait_ge(zeroed, Z_HIDDEN - 3)
            gp.memset(sh[0:96, :, QI - 1, :], 0.0).then_inc(zeroed, 1)
            gp.wait_ge(zeroed, Z_HIDDEN - 2)
            gp.memset(sh[0:96, :, :, 0], 0.0).then_inc(zeroed, 1)
            gp.wait_ge(zeroed, Z_HIDDEN - 1)
            gp.memset(sh[0:96, :, :, W - 1], 0.0).then_inc(zeroed, 1)
            gp.wait_ge(zeroed, Z_HIDDEN)
            gp.wait_ge(bn_input_ready, 1)
            gp.tensor_tensor(Q2[:, 7, 1:2], Q2[:, 7, 0:1], MHALF[:, 0:1], ALU.pow).then_inc(bn_power_done, 1)
            gp.wait_ge(bn_input_ready, 4)
            gp.tensor_tensor(Q2[:, 4, :], Q2[:, 3, :], MHALF[:, :], ALU.pow).then_inc(bn_power_done, 1)
            gp.wait_ge(masked_conv2_done, NE)
            clear_pads(1)
            gp.wait_ge(norm2_done, 1)
            for e in range(NE):
                gp.wait_ge(z_done, e + 1)
                gp.tensor_tensor(T2[e][:, 0:6 * W], U[:, 0:6 * W], Z[:, e, 0:6 * W], ALU.add)
                gp.tensor_tensor(T2[e][:, 6 * W:7 * W], U[:, (H - 1) * W:PIX], Z[:, e, 7 * W:8 * W], ALU.add).then_inc(first_rows_added, 1)
            xp = X[:, (H - 1 - PROWS) * W:(H - 1) * W].rearrange("p (r c) -> p r c", c=W)[:, :, 1:W - 1]
            for e in range(NE):
                gp.wait_ge(pool_relu_done, e + 1)
                if e:
                    gp.wait_ge(pool_rows_added, e)
                gp.tensor_tensor(xp, xp, RR[e % 2][:, :].rearrange("p (r c) -> p r c", c=W - 2), ALU.add).then_inc(pool_rows_added, 1)
            rstd(4)

        @block.scalar
        def _(act):
            act.wait_ge(zeroed, Z_BORDER)
            def hi(k):
                act.wait_ge(norm0_done, k + 1)
                act.activation(rows(HI, 1 + k * CR, CR), U[:, k * CH:(k + 1) * CH].rearrange("p (r c) -> p r c", c=W), ACT.Copy).then_inc(hi_done, 1)

            hi(0)
            hi(1)
            act.wait_ge(w_par, 16)
            for k in range(NCH):
                act.wait_ge(pw_conv_done, k + 1)
                act.activation(rows(P1[0:64, :], 1 + k * CR, CR), pw_bank(k)[0:64, :].rearrange("p (r c) -> p r c", c=W), ACT.Relu,
                               bias=PAR[0:64, PB:PB + 1]).then_inc(p1_lower_done, 1)
                if k + 2 < NCH:
                    hi(k + 2)
            for q in range(4):
                act.wait_ge(para_conv_done, q + 1)
                act.activation(para_rows(q, 0), ps[4 + q % 2][0:64, :].rearrange("p (r c) -> p r c", c=W), ACT.Identity,
                               bias=PAR[0:64, CB:CB + 1]).then_inc(para_even_done, 1)
            with act.Fori(0, STEPS) as it:
                for pair in range(STRIP_T):
                    act.wait_ge(sums_transposed, it * TIT + 2 * pair + 2)
                    act.activation(P1[:, bass.ds(it * 2 * SL + pair * 2 * P, 2 * P)], pair_bank(pair), ACT.Copy).then_inc(block0_in_sbuf, 1)
            for pair in range(2):
                g = STEPS * TIT + 2 * pair
                n = min(2, NT - g)
                act.wait_ge(sums_transposed, g + n)
                act.activation(P1[:, g * P:(g + n) * P], pair_bank(pair)[:, 0:n * P], ACT.Copy).then_inc(block0_in_sbuf, 1)

            def norm(out_ap, k0, k1, p=slice(0, P), c0=0, c1=W):
                return act.activation(out_ap, X[p, k0 * W:k1 * W].rearrange("p (r c) -> p r c", c=W)[:, :, c0:c1], ACT.Identity,
                                      bias=NMR[p, 0:1], scale=RS[p, 0:1])

            def image_and_stack(base, groups, first_rows, share, own):
                act.wait_ge(coef_ready, base)
                for k in (3, 5):
                    norm(rows(IMG, 1 + k * CR, CR), k * CR, (k + 1) * CR).then_inc(image_by_scalar, 1)
                act.wait_ge(stack_pads_zeroed, 3 if groups == 4 else 6)
                for n, (r0, r1) in enumerate(((0, first_rows), (first_rows, first_rows + CR))):
                    for b, g in share:
                        pixel0, col0, width = span(g)
                        ins = norm(SK[32 * g:32 * g + 32, b, (1 + r0) * PW:(1 + r1) * PW].rearrange("p (r c) -> p r c", c=PW)[:, :, col0:col0 + width],
                                   r0, r1, slice(32 * b, 32 * b + 32), pixel0, pixel0 + width)
                    ins.then_inc(own, 1)
                    if n == 0:
                        norm(rows(IMG, 1 + 7 * CR, CR), 7 * CR, 8 * CR).then_inc(image_by_scalar, 1)

            image_and_stack(1, 4, CR + 2, SHARE4_A, stack1_by_scalar)
            act.wait_ge(coef_ready, 2)
            act.wait_ge(zeroed, Z_LATER)
            for b, g in SHARE3_A:
                pixel0, col0, width = span(g)
                ins = norm(CS[32 * g:32 * g + 32, b, W:5 * W].rearrange("p (r c) -> p r c", c=W)[:, :, col0:col0 + width],
                           0, 4, slice(32 * b, 32 * b + 32), pixel0, pixel0 + width)
            ins.then_inc(compact_by_scalar, 1)
            act.activation(U[:, :], X[:, :], ACT.Identity, bias=NMR[:, 0:1], scale=RS[:, 0:1]).then_inc(norm2_done, 1)
            act.wait_ge(bn1_ready, 1)
            for b in (1, 3):
                act.activation(H1[:, b, 0:5 * W], ps[b][:, 0:5 * W], ACT.Relu, bias=Q2[:, 7, 3:4], scale=Q2[:, 7, 2:3]).then_inc(hidden_by_scalar, 1)
            act.wait_ge(hidden_by_vector, 3)
            act.wait_ge(hidden_by_scalar, 2)
            act.wait_ge(zeroed, Z_HIDDEN)
            for e in range(NE):
                act.activation(*hidden_copy(e, 0), ACT.Copy).then_inc(hidden_stack_by_scalar, 1)
            act.wait_ge(bn2_ready, 1)
            for e in range(NE):
                act.wait_ge(z_row6_done, e + 1)
                act.activation(Z[:, e, :], ps[e][:, :], ACT.Identity, bias=Q2[:, 6, e:e + 1], scale=Q2[:, 5, e:e + 1]).then_inc(z_done, 1)
            act.wait_ge(minus_z_ready, 1)
            up = U[:, (H - 1 - PROWS) * W:(H - 1) * W].rearrange("p (r c) -> p r c", c=W)[:, :, 1:W - 1]
            for e in range(NE):
                if e >= 2:
                    act.wait_ge(pool_rows_added, e - 1)
                act.activation(RR[e % 2][:, :].rearrange("p (r c) -> p r c", c=W - 2), up, ACT.Relu, bias=Z6[:, e, 1:2]).then_inc(pool_relu_done, 1)
            act.wait_ge(max_sum_done, 1)
            xe = X[:, 6 * W:(H - 1) * W].rearrange("p (r c) -> p r c", c=W)
            act.activation(xe[:, :, 0:1], xe[:, :, 0:1], ACT.Identity, bias=AS[:, 0:1]).then_inc(z_sum_added, 1)
            act.activation(xe[:, :, W - 1:W], xe[:, :, W - 1:W], ACT.Identity, bias=AS[:, 2:3]).then_inc(z_sum_added, 1)
            for i, (r0, r1) in enumerate(PARTS):
                act.wait_ge(max_sum_done, i + 1)
                xh = X[:, r0 * W:r1 * W].rearrange("p (r c) -> p r c", c=W)[:, :, 1:W - 1]
                act.activation(xh, xh, ACT.Identity, bias=AS[:, 1:2]).then_inc(z_sum_added, 1)
            image_and_stack(3, 3, CR + 1, SHARE3_A, stack3_by_scalar)
            act.wait_ge(w3_mixed, 1)
            act.wait_ge(zeroed, Z_LATER)
            for k in range(NCH):
                act.wait_ge(conv3_done, k + 1)
                act.activation(rows(IMG2, 1 + k * CR, CR), ps[k % 4][:, :].rearrange("p (r c) -> p r c", c=W), ACT.Relu,
                               bias=S3[:, 1:2], scale=S3[:, 0:1]).then_inc(hidden3_done, 1)
            act.wait_ge(image_by_vector, 7)
            act.wait_ge(stack3_by_vector, 2)
            act.wait_ge(stack3_by_scalar, 2)
            act.activation(X[:, :], X[:, :], ACT.Identity, bias=S3[:, 3:4]).then_inc(x3_shifted, 1)

        @block.tensor
        def _(pe):
            pe.wait_ge(w_pw, 64)
            for k in range(NCH):
                pe.wait_ge(norm0_done, k + 1)
                if k >= 4:
                    pe.wait_ge(p1_lower_done, k - 3)
                    pe.wait_ge(p1_upper_done, k - 3)
                pe.matmul(pw_bank(k)[:, :], PWB[:, :, :, :], U[:, k * CH:(k + 1) * CH], start=True, stop=True).then_inc(pw_conv_done, 1)
            pe.wait_ge(w_cw, 16 * 6 * B)
            for q in range(4):
                pe.wait_ge(p1_lower_done, min(2 * q + 3, NCH))
                pe.wait_ge(p1_upper_done, min(2 * q + 3, NCH))
                if q >= 2:
                    pe.wait_ge(para_even_done, q - 1)
                    pe.wait_ge(para_odd_done, q - 1)
                for i in range(6):
                    a = (16 * q + i // 3 * 2) * PW
                    ins = pe.matmul(ps[4 + q % 2][:, :], CWB[:, i, :, :, :],
                                    P1[:, a:a + 16 * PW].rearrange("p (r h c) -> p r h c", h=2, c=PW)[:, :, 0, i % 3:i % 3 + W],
                                    start=(i == 0), stop=(i == 5))
                ins.then_inc(para_conv_done, 1)
            pe.wait_ge(para_pads, 1)
            for q in range(5):
                pe.wait_ge(para_even_done, min(q + 1, 4))
                pe.wait_ge(para_odd_done, min(q + 1, 4))
                if q >= 2:
                    pe.wait_ge(pt_in_sbuf, q - 1)
                for t in range(8 if q < 4 else 1):
                    a = (8 * q + t) * P
                    ins = pe.transpose(ps[6 + q % 2][:, t * 64:(t + 1) * 64], PARA[:, a:a + P], ID[0:64, 0:64])
                ins.then_inc(pt_done, 1)

            def tile(half, t, b):
                px = lambda s, off, k=P: s[half][0:k, b, off + t * P:off + (t + 1) * P]
                for dy in range(3):
                    pe.matmul(ps[b][:, :], px(HS, dy * PW), WA[:, dy, :], start=(dy == 0), stop=False)
                    pe.matmul(ps[b][:, :], px(LS, dy * PW), WB[:, dy, :], start=False, stop=False)
                pe.matmul(ps[b][:, :], px(TS, 0, 96), WC[:, :], start=False, stop=True).then_inc(tile_done, 1)

            def back(j, g, it=0):
                pe.wait_ge(sum_done, 4 * g + 4)
                first = isinstance(it, int) and it == 0
                if j == 8:
                    pe.wait_ge(block0_in_sbuf, STRIP_T * it + 1)
                elif j == 0 and not first:
                    pe.wait_ge(block0_in_sbuf, STRIP_T * it)
                elif j % 2 == 0 and not first:
                    pe.wait_ge(block0_in_sbuf, STRIP_T * (it - 1) + j // 2 + 1)
                pe.transpose(pair_bank(j // 2)[:, j % 2 * P:(j % 2 + 1) * P], RED[j % 2][:, :], ID[:, :]).then_inc(sums_transposed, 1)

            def block0(it, tiles, first=False):
                for j in range(tiles):
                    half, t = j // STRIP_T, j % STRIP_T
                    g = it * TIT + j
                    if t == 0:
                        pe.wait_ge(strip_ready[half], 16 * NDMA * (it + 1))
                    for b in range(B):
                        if not (first and j == 0):
                            pe.wait_ge(product_done, 4 * g + b - 3)
                        tile(half, t, b)
                    if j > 0:
                        back(j - 1, g - 1, it)
                    elif not first:
                        back(TIT - 1, g - 1)

            pe.wait_ge(w0_split, 4)
            block0(0, TIT, True)
            with pe.Fori(1, STEPS) as it:
                block0(it, TIT)
            block0(STEPS, REST)
            back(REST - 1, NT - 1, STEPS)

            def conv(k, wt, slots, done):
                for y in range(slots):
                    for b in range(B):
                        ins = pe.matmul(ps[k % 4][32 * b:32 * b + 32, :], wt(y), rows(SK[:, b, :], k * CR + y, CR, 0),
                                        start=(y == 0), stop=(y == slots - 1))
                ins.then_inc(done, 1)

            def engine_rows(k, ev, ea):
                if k < 2:
                    pe.wait_ge(ev, k + 1)
                    pe.wait_ge(ea, k + 1)

            pe.wait_ge(far_known, 1)
            far = pe.value_load(FARN[0:1, 0:1], min_val=0, max_val=1)
            with pe.If(far > 0):
                with pe.Fori(0, TAPS) as tap:
                    with pe.Fori(0, NCH) as k:
                        pe.wait_ge(far_window, tap * NCH + k + 1)
                        for s in range(4):
                            ins = pe.matmul(ps[7][:, :], FB[:, s, :], FW[:, s // 2:s // 2 + CR, s % 2:s % 2 + W], start=(s == 0), stop=(s == 3))
                        ins.then_inc(far_conv, 1)
            pe.wait_ge(w1_mixed, 1)
            for k in range(NCH):
                engine_rows(k, stack1_by_vector, stack1_by_scalar)
                if k in (2, 5):
                    pe.wait_ge(stack1_by_dma[k // 5], 16 * 16)
                if k >= 4:
                    pe.wait_ge(x2_done, k - 3)
                conv(k, lambda y: WE[:, y, :], 4, conv1_done)
            pe.wait_ge(w_l2, 32)
            pe.wait_ge(compact_by_vector, 1)
            pe.wait_ge(compact_by_scalar, 1)
            for b in range(B):
                for dy in range(3):
                    ins = pe.matmul(ps[b][:, 0:5 * W], W2A[:, dy, :], CS[:, b, dy * W:(dy + 5) * W], start=(dy == 0), stop=(dy == 2))
                ins.then_inc(masked_conv1_done, 1)
            for e in range(NE):
                pe.wait_ge(hidden_stack_by_vector, 2 * e + 2)
                pe.wait_ge(hidden_stack_by_scalar, e + 1)
                for dy in range(3):
                    for b in range(B):
                        ins = pe.matmul(ps[e][32 * b:32 * b + 32, :], W2B[:, e, dy, :], SH[:, e, b, dy * W:(dy + CROWS) * W],
                                        start=(dy == 0), stop=(dy == 2))
                ins.then_inc(masked_conv2_done, 1)
            for i, q in ((0, 0), (1, 2)):
                pe.wait_ge(bn_input_ready, 2 + i)
                pe.matmul(ps[4][:, 8 * i:8 * i + NE], AVG[:, :, :], Q2[:, q, :], start=True, stop=True).then_inc(averaged, 1)
            pe.wait_ge(w3_mixed, 1)
            for k in range(NCH):
                engine_rows(k, stack3_by_vector, stack3_by_scalar)
                if k in (2, 5):
                    pe.wait_ge(stack3_by_dma[k // 5], 16 * 12)
                if k >= 4:
                    pe.wait_ge(hidden3_done, k - 3)
                conv(k, lambda y: W3A[:, 32 * y:32 * y + 32], 3, conv3_done)
            for k in range(NCH):
                if k in (0, 2, 5):
                    pe.wait_ge(stack4_by_dma[(k + 1) // 3], 16 * 12)
                pe.wait_ge(hidden3_done, min(5 + k, NCH))
                if k >= 4:
                    pe.wait_ge(affine4_done, k - 3)
                conv(k, lambda y: W3B[:, 32 * y:32 * y + 32], 3, conv4_done)

        @block.vector
        def _(ve):
            n = [0]

            def step(ins):
                n[0] += 1
                ins.then_inc(vector_step, 1)
                ve.wait_ge(vector_step, n[0])

            def coefs(k):
                step(ve.bn_aggr(MV[:, :], ST[:, :, :]))
                ve.tensor_scalar(VE[:, :], MV[:, 1:2], EPS, None, ALU.add).then_inc(var_ready, 1)
                ve.wait_ge(rstd_ready, k)
                ins = ve.scalar_tensor_tensor(NMR[:, :], MV[:, 0:1], -1.0, RS[:, :], ALU.mult, ALU.mult)
                if k > 1:
                    ins.then_inc(coef_ready, 1)

            for k in range(NCH):
                if k % 2 == 0:
                    ve.wait_ge(x_in[k // 2], 16)
                ins = ve.bn_stats(ST[:, k, :], X[:, k * CH:(k + 1) * CH])
            step(ins)
            coefs(1)
            for k in range(NCH):
                ve.tensor_scalar(U[:, k * CH:(k + 1) * CH], X[:, k * CH:(k + 1) * CH], MV[:, 0:1], RS[:, 0:1], ALU.subtract, ALU.mult).then_inc(norm0_done, 1)
            ve.wait_ge(w_par, 16)
            for k in range(NCH):
                ve.wait_ge(pw_conv_done, k + 1)
                ve.tensor_scalar(rows(P1[64:128, :], k * CR, CR), pw_bank(k)[64:128, :].rearrange("p (r c) -> p r c", c=W),
                                 PAR[64:128, PB:PB + 1], 0.0, ALU.add, ALU.max).then_inc(p1_upper_done, 1)
            ve.wait_ge(w_main, 64)
            ve.tensor_copy(WA[:, :, :], RA[:, :, :]).then_inc(w0_split, 1)
            ve.wait_ge(w0_split, 1)
            ve.tensor_tensor(WB[0:96, :, :], RA[0:96, :, :], WA[0:96, :, :].bitcast(F32), ALU.subtract).then_inc(w0_split, 1)
            ve.tensor_copy(WB[96:128, :, :], WA[32:64, :, :]).then_inc(w0_split, 1)
            for dy in range(3):
                ins = ve.tensor_copy(WC[32 * dy:32 * dy + 32, :], WA[64:96, dy, :])
            ins.then_inc(w0_split, 1)
            ve.wait_ge(w0_split, 4)
            for q in range(4):
                ve.wait_ge(para_conv_done, q + 1)
                ve.tensor_scalar(para_rows(q, 1), ps[4 + q % 2][64:128, :].rearrange("p (r c) -> p r c", c=W),
                                 PAR[64:128, CB:CB + 1], None, ALU.add).then_inc(para_odd_done, 1)
            for q in range(5):
                ve.wait_ge(pt_done, q + 1)
                n_pt = CH if q < 4 else 64
                ve.tensor_copy(PT[:, q * CH:q * CH + n_pt], ps[6 + q % 2][:, 0:n_pt]).then_inc(pt_in_sbuf, 1)
            ve.wait_ge(pt_in_sbuf, 5)

            def reduce(j, b, m):
                ve.wait_ge(product_done, m + 1)
                ve.tensor_reduce(RED[j % 2][:, 32 * b:32 * b + 32], PROD[b % 2][:, :].rearrange("p (o e) -> p o e", e=E0), AX.X, ALU.add).then_inc(sum_done, 1)

            def finish_chunk(k):
                ve.wait_ge(block0_in_sbuf, 2 * k + 3)
                xs = X[:, bass.ds(k * CH, CH)].rearrange("p (r c) -> p r c", c=W)
                d = P1[:, bass.ds(k * (CR * PW), CR * PW)].rearrange("p (r c) -> p r c", c=PW)[:, :, 0:W]
                ve.tensor_tensor(xs, d, xs, ALU.add).then_inc(x1_done, 1)
                ve.wait_ge(x1_done, k + 1)
                ve.bn_stats(ST[:, bass.ds(k, 1), :], xs).then_inc(stats1_done, 1)

            def product(b, g):
                m = 4 * g + b
                ve.wait_ge(tile_done, m + 1)
                if not isinstance(m, int) or m >= 2:
                    ve.wait_ge(sum_done, m - 1)
                para = PT[:, bass.ds(g * (B * E0) + b * E0, E0)]
                ve.tensor_tensor(PROD[b % 2][:, :].rearrange("p (o e) -> p o e", e=E0), ps[b][:, :].rearrange("p (o e) -> p o e", e=E0),
                                 para.rearrange("p (a e) -> p a e", a=1).broadcast_to([P, C, E0]), ALU.mult).then_inc(product_done, 1)

            def block0(it, tiles, finish, first=False):
                for j in range(tiles):
                    g = it * TIT + j
                    for b in range(B):
                        product(b, g)
                        if b > 0:
                            if b == 1 and not (first and j < 2):
                                ve.wait_ge(sums_transposed, g - 1)
                            reduce(j, b - 1, 4 * g + b - 1)
                        elif not (first and j == 0):
                            reduce((j - 1) % 2, 3, 4 * g - 1)
                    if j in finish:
                        finish_chunk(finish[j])

            block0(0, TIT, {8: 0}, True)
            with ve.Fori(1, STEPS) as it:
                block0(it, TIT, {3: 2 * it - 1, 8: 2 * it})
            block0(STEPS, REST, {0: 2 * STEPS - 1, 1: 2 * STEPS})
            reduce(REST - 1, 3, 4 * NT - 1)
            finish_chunk(NCH - 1)
            ve.wait_ge(stats1_done, NCH)

            def norm(out_ap, k0, k1, p=slice(0, P), c0=0, c1=W):
                return ve.tensor_scalar(out_ap, X[p, k0 * W:k1 * W].rearrange("p (r c) -> p r c", c=W)[:, :, c0:c1],
                                        MV[p, 0:1], RS[p, 0:1], ALU.subtract, ALU.mult)

            def image_and_stack(groups, first_rows, share, own, whole):
                for k in (2, 4):
                    norm(rows(IMG, 1 + k * CR, CR), k * CR, (k + 1) * CR).then_inc(image_by_vector, 1)
                ve.wait_ge(stack_pads_zeroed, 3 if groups == 4 else 6)
                for n, (r0, r1) in enumerate(((0, first_rows), (first_rows, first_rows + CR))):
                    for b, g in share:
                        pixel0, col0, width = span(g)
                        ins = norm(SK[32 * g:32 * g + 32, b, (1 + r0) * PW:(1 + r1) * PW].rearrange("p (r c) -> p r c", c=PW)[:, :, col0:col0 + width],
                                   r0, r1, slice(32 * b, 32 * b + 32), pixel0, pixel0 + width)
                    ins.then_inc(own, 1)
                    if n == 0:
                        norm(rows(IMG, 1 + 6 * CR, CR), 6 * CR, 7 * CR).then_inc(image_by_vector, 1)
                if whole:
                    norm(rows(IMG, 1, 2 * CR), 0, 2 * CR).then_inc(image_by_vector, 1)

            coefs(2)
            image_and_stack(4, CR + 2, SHARE4_V, stack1_by_vector, False)
            ve.wait_ge(stack1_by_vector, 2)
            ve.wait_ge(stack1_by_scalar, 2)
            ve.wait_ge(image_by_vector, 3)
            ve.wait_ge(image_by_scalar, 3)
            ve.wait_ge(far_known, 1)
            far = ve.value_load(FARN[0:1, 0:1], min_val=0, max_val=1)
            with ve.If(far > 0):
                ve.memset(FE[:, :], 0.0).then_inc(far_image, 1)
                ve.memset(FS[:, :, :], 0.0).then_inc(far_image, 1)
                ve.memset(FB[:, :, :], 0.0).then_inc(far_image, 1)
                ve.wait_ge(far_image, 3)
                norm(rows(FE, FAR + 1, H), 0, H).then_inc(far_image, 1)
                ve.wait_ge(far_image, 4)
                with ve.Fori(0, TAPS) as tap:
                    row0 = ve.value_load(OFI[0:1, bass.ds(tap, 1)], min_val=0, max_val=2 * FAR)
                    col0 = ve.value_load(OFI[0:1, bass.ds(tap + TAPS, 1)], min_val=0, max_val=2 * FAR)
                    for b in range(B):
                        p = slice(32 * b, 32 * b + 32)
                        for s in range(4):
                            ins = ve.tensor_tensor(FB[p, s:s + 1, 32 * b:32 * b + 32].rearrange("p a o -> p o a"), W1R[p, :, bass.ds(tap, 1)],
                                                   FC[p, s:s + 1, bass.ds(tap, 1)].broadcast_to([C, C, 1]), ALU.mult)
                    ins.then_inc(far_weights, 1)
                    with ve.Fori(0, NCH) as k:
                        ve.wait_ge(far_weights, tap + 1)
                        ve.tensor_copy(FS[:, :, FAR + 1:FAR + 1 + PW],
                                       FE[:, bass.ds((row0 + k * CR) * PW, (CR + 1) * PW)].rearrange("p (r c) -> p r c", c=PW)).then_inc(far_strip, 1)
                        ve.wait_ge(far_strip, tap * NCH + k + 1)
                        ve.tensor_copy(FW[:, :, :], FS[:, :, bass.ds(col0 + 1, W + 1)]).then_inc(far_window, 1)
                        ve.wait_ge(far_conv, tap * NCH + k + 1)
                        xs = X[:, bass.ds(k * CH, CH)]
                        ve.tensor_tensor(xs, ps[7][:, :], xs, ALU.add).then_inc(far_added, 1)
                        ve.wait_ge(far_added, tap * NCH + k + 1)
                ve.memset(CX[:, :], 0.0).then_inc(far_over, 1)
            for k in range(NCH):
                ve.wait_ge(conv1_done, k + 1)
                xs = X[:, k * CH:(k + 1) * CH]
                ve.tensor_tensor(xs, ps[k % 4][:, :], xs, ALU.add).then_inc(x2_done, 1)
                ve.wait_ge(x2_done, k + 1)
                ins = ve.bn_stats(ST[:, k, :], xs)
            step(ins)
            coefs(3)
            ve.wait_ge(zeroed, Z_LATER)
            for b, g in SHARE3_V:
                pixel0, col0, width = span(g)
                ins = norm(CS[32 * g:32 * g + 32, b, W:5 * W].rearrange("p (r c) -> p r c", c=W)[:, :, col0:col0 + width],
                           0, 4, slice(32 * b, 32 * b + 32), pixel0, pixel0 + width)
            ins.then_inc(compact_by_vector, 1)
            step(ve.memset(S1[:, 4, :], 0.0))
            step(ve.memset(S1[:, 4, 0:6:3], (NPIX - B * 5 * W) / 2.0))
            for b in range(B):
                ve.wait_ge(masked_conv1_done, b + 1)
                ins = ve.bn_stats(S1[:, b, :], ps[b][:, 0:5 * W])
            step(ins)
            step(ve.bn_aggr(M2[:, 0, :], S1[:, :, :]))
            ve.tensor_scalar(Q2[:, 7, 0:1], M2[:, 0, 1:2], EPS, None, ALU.add).then_inc(bn_input_ready, 1)
            step(ve.tensor_tensor(M2[:, 1, 0:1], M2[:, 0, 0:1], PAR[:, B1:B1 + 1], ALU.add))
            step(ve.tensor_tensor(M2[:, 1, 1:2], PAR[:, B1:B1 + 1], M2[:, 1, 0:1], ALU.subtract))
            ve.wait_ge(bn_power_done, 1)
            step(ve.tensor_tensor(Q2[:, 7, 2:3], Q2[:, 7, 1:2], PAR[:, G1:G1 + 1], ALU.mult))
            ve.scalar_tensor_tensor(Q2[:, 7, 3:4], M2[:, 1, 1:2], Q2[:, 7, 2:3], PAR[:, BE1:BE1 + 1], ALU.mult, ALU.add).then_inc(bn1_ready, 1)
            ve.wait_ge(bn1_ready, 1)
            for b in (0, 2):
                step(ve.tensor_scalar(H1[:, b, 0:5 * W], ps[b][:, 0:5 * W], Q2[:, 7, 2:3], Q2[:, 7, 3:4], ALU.mult, ALU.add))
                ve.tensor_scalar(H1[:, b, 0:5 * W], H1[:, b, 0:5 * W], 0.0, None, ALU.max).then_inc(hidden_by_vector, 1)
            ve.tensor_scalar(H1[:, :, 5 * W:CROWS * W], Q2[:, 7, 3:4].rearrange("p (a c) -> p a c", a=1).broadcast_to([P, B, 3 * W]), 0.0, None, ALU.max).then_inc(hidden_by_vector, 1)
            ve.wait_ge(hidden_by_vector, 3)
            ve.wait_ge(hidden_by_scalar, 2)
            ve.wait_ge(zeroed, Z_HIDDEN)
            for e in range(NE):
                for g in (1, 2):
                    ve.tensor_copy(*hidden_copy(e, g)).then_inc(hidden_stack_by_vector, 1)
            for e in range(NE):
                ve.wait_ge(masked_conv2_done, e + 1)
                ve.bn_stats(S2[:, e, 0, :], ps[e][:, 0:6 * W])
                ve.bn_stats(S2[:, e, 1, :], ps[e][:, 6 * W:7 * W])
                ins = ve.bn_stats(S2[:, e, 2, :], ps[e][:, 7 * W:8 * W])
            step(ins)
            for i in (0, 2, 3, 5):
                ins = ve.tensor_scalar(S2[:, :, 1, i:i + 1], S2[:, :, 1, i:i + 1], float(REP), None, ALU.mult)
            step(ins)
            for e in range(NE):
                ins = ve.bn_aggr(M2[:, e, :], S2[:, e, :, :])
            step(ins)
            ve.tensor_copy(Q2[:, 0, :], M2[:, :, 0]).then_inc(bn_input_ready, 1)
            ve.wait_ge(averaged, 1)
            step(ve.tensor_copy(Q2[:, 1, :], ps[4][:, 0:NE]))
            step(ve.tensor_tensor(Q2[:, 2, :], Q2[:, 0, :], Q2[:, 1, :], ALU.subtract))
            step(ve.tensor_tensor(Q2[:, 2, :], Q2[:, 2, :], Q2[:, 2, :], ALU.mult))
            ve.tensor_tensor(Q2[:, 2, :], Q2[:, 2, :], M2[:, :, 1], ALU.add).then_inc(bn_input_ready, 1)
            ve.wait_ge(averaged, 2)
            ve.tensor_scalar(Q2[:, 3, :], ps[4][:, 8:8 + NE], EPS, None, ALU.add).then_inc(bn_input_ready, 1)
            step(ve.tensor_tensor(Q2[:, 1, :], Q2[:, 1, :], PAR[:, B2:B2 + NE], ALU.add))
            step(ve.tensor_tensor(Q2[:, 1, :], PAR[:, B2:B2 + NE], Q2[:, 1, :], ALU.subtract))
            ve.wait_ge(bn_power_done, 2)
            step(ve.tensor_tensor(Q2[:, 5, :], Q2[:, 4, :], PAR[:, G2:G2 + NE], ALU.mult))
            step(ve.tensor_tensor(Q2[:, 6, :], Q2[:, 1, :], Q2[:, 5, :], ALU.mult))
            ve.tensor_tensor(Q2[:, 6, :], Q2[:, 6, :], PAR[:, BE2:BE2 + NE], ALU.add).then_inc(bn2_ready, 1)
            ve.wait_ge(bn2_ready, 1)
            for e in range(NE):
                ins = ve.tensor_scalar(Z6[:, e, :], ps[e][:, 6 * W:7 * W], Q2[:, 5, e:e + 1], Q2[:, 6, e:e + 1], ALU.mult, ALU.add).then_inc(z_row6_done, 1)
            ve.wait_ge(z_row6_done, NE)
            for j, c in enumerate((0, 1, W - 1)):
                ins = ve.tensor_scalar(NA[:, :, j], Z6[:, :, c], -1.0, None, ALU.mult)
            ins.then_inc(minus_z_ready, 1)
            ve.wait_ge(minus_z_ready, 1)
            ve.wait_ge(norm2_done, 1)
            (r0, r1), (r2, r3) = PARTS
            body = lambda m, a, b, c0, c1: m[:, a * W:b * W].rearrange("p (r c) -> p r c", c=W)[:, :, c0:c1]

            def add_max(e, j, a, b, c0, c1):
                return ve.scalar_tensor_tensor(body(X, a, b, c0, c1), body(U, a, b, c0, c1), NA[:, e, j:j + 1], body(X, a, b, c0, c1), ALU.max, ALU.add)

            for e in range(NE):
                add_max(e, 0, 6, H - 1, 0, 1)
                add_max(e, 2, 6, H - 1, W - 1, W)
                if e == 0:
                    for j in range(3):
                        ins = ve.tensor_reduce(AS[:, j:j + 1], NA[:, :, j], AX.X, ALU.add, negate=True)
                ins = add_max(e, 1, r0, r1, 1, W - 1)
                if e < NE - 1:
                    step(ins)
            ins.then_inc(max_sum_done, 1)
            for e in range(NE):
                ve.wait_ge(first_rows_added, e + 1)
                for a, m, t0 in ((0, 6 * W, 0), ((H - 1) * W, W, 6 * W)):
                    ve.scalar_tensor_tensor(X[:, a:a + m], T2[e][:, t0:t0 + m], 0.0, X[:, a:a + m], ALU.max, ALU.add)
                ins = add_max(e, 1, r2, r3, 1, W - 1)
                if e < NE - 1:
                    step(ins)
            ins.then_inc(max_sum_done, 1)
            ve.wait_ge(max_sum_done, 2)
            ve.wait_ge(z_sum_added, 3)
            for k in range(0, 3):
                ve.bn_stats(ST[:, k, :], X[:, k * CH:(k + 1) * CH])
            ve.wait_ge(z_sum_added, 4)
            ve.wait_ge(pool_rows_added, NE)
            for k in range(3, NCH):
                ins = ve.bn_stats(ST[:, k, :], X[:, k * CH:(k + 1) * CH])
            step(ins)
            coefs(4)
            image_and_stack(3, CR + 1, SHARE3_V, stack3_by_vector, True)
            ve.wait_ge(image_by_vector, 7)
            ve.wait_ge(image_by_scalar, 6)
            for k in range(NCH):
                ve.wait_ge(conv4_done, k + 1)
                ve.scalar_tensor_tensor(T2[k % 4][:, :].rearrange("p (r c) -> p r c", c=W), ps[k % 4][:, :].rearrange("p (r c) -> p r c", c=W),
                                        S3[:, 2:3], rows(IMG, 1 + k * CR, CR), ALU.mult, ALU.add).then_inc(affine4_done, 1)
                ve.wait_ge(affine4_done, k + 1)
                if k == 0:
                    ve.wait_ge(x3_shifted, 1)
                if k >= 4:
                    ve.wait_ge(out_written[k % 4], 16 * (k // 4))
                ve.scalar_tensor_tensor(OT[k % 4][:, :], T2[k % 4][:, :], S3[:, 4:5], X[:, k * CH:(k + 1) * CH], ALU.max, ALU.add).then_inc(out_rows_done, 1)


def kernel(**inputs):
    import numpy as np
    import concourse.bacc as bacc
    from concourse.bass_utils import run_bass_kernel_spmd as run

    g = {k: np.asarray(v) for k, v in inputs.items()}
    col = lambda a: np.tile(a, P // a.size).reshape(P, 1)
    row = lambda a: np.broadcast_to(a.reshape(1, -1), (P, a.size))
    eo = lambda a: np.tile(a.T, (B, 1))
    par = np.concatenate(
        [col(g['L0_conv_pb']), col(g['L0_conv_cb'])]
        + [g['L2_conv_' + n].reshape(P, 1) for n in ('b1', 'gamma1', 'beta1')]
        + [eo(g['L2_conv_' + n]) for n in ('b2', 'gamma2', 'beta2')]
        + [col(g['L3_conv_bn%d_%s' % (i, n)]) for i in (1, 2) for n in ('gamma', 'beta', 'mean', 'var')]
        + [row(g['L3_conv_alpha']), row(g['L1_conv_tap_offsets'][:, 0]), row(g['L1_conv_tap_offsets'][:, 1])], axis=1)
    arrays = {
        'x': g['x'].reshape(P, PIX),
        'w0': g['L0_conv_W'].reshape(C, C, TAPS, E0).transpose(2, 1, 0, 3).reshape(TAPS, C, C * E0),
        'pw': np.broadcast_to(g['L0_conv_pw'].reshape(E0, C).T[:, None, :], (C, 2, E0)),
        'cw': g['L0_conv_cw'].transpose(1, 2, 3, 0),
        'w1': g['L1_conv_weights'].transpose(1, 0, 2),
        'w2a': g['L2_conv_w1'].transpose(4, 2, 3, 0, 1).reshape(96, 3, NE * C),
        'w2b': g['L2_conv_w2'].transpose(4, 2, 0, 3, 1).reshape(96, NE, 3, C),
        'w3a': g['L3_conv_w1'].transpose(4, 2, 0, 3, 1).reshape(96, NM, 3 * C),
        'w3b': g['L3_conv_w2'].transpose(4, 2, 0, 3, 1).reshape(96, NM, 3 * C),
        'par': par,
    }
    nc = bacc.Bacc("TRN2", target_bir_lowering=False, num_devices=1)
    ins, args = {}, []
    for name, a in arrays.items():
        ins['in_' + name] = np.ascontiguousarray(a)
        args.append(nc.dram_tensor('in_' + name, a.shape, F32, kind="ExternalInput").ap())
    args.append(nc.dram_tensor("out_x", (P, PIX), F32, kind="ExternalOutput").ap())
    build(nc, *args)
    r = run(nc, [ins], core_ids=[0])
    return r.results[0]["out_x"].reshape(B, C, H, W)
```
